# Optimizing a Trainium2 kernel written in Bass

```python
import numpy as np
import jax
import jax.numpy as jnp

def _softmax(x, axis=-1):
    return jax.nn.softmax(x, axis=axis)

def _gelu(x):
    return jax.nn.gelu(x, approximate=True)

def _silu(x):
    return jax.nn.silu(x)

def _sigmoid(x):
    return jax.nn.sigmoid(x)

def _layernorm(x, axis=-1, eps=1e-05):
    m = jnp.mean(x, axis=axis, keepdims=True)
    v = jnp.var(x, axis=axis, keepdims=True)
    return (x - m) / jnp.sqrt(v + eps)

def _scatter_add(tgt, idx, src, axis=0):
    return tgt.at[idx].add(src)

def _segment_sum(src, seg, n):
    return jax.ops.segment_sum(src, seg, n)
kernel_name = 'mk_recurrent_d1_jaxref_r8_e9e358'

def setup_inputs(seed: int=0):
    np.random.seed(seed)
    _w = jnp.asarray

    def _L0_attn_setup():
        import jax, jax.numpy as jnp
        import numpy as np
        D_MODEL = 128
        NUM_HEADS = 16
        HEAD_DIM = D_MODEL // NUM_HEADS
        WINDOW = 128
        SCALE = HEAD_DIM ** (-0.5)
        key = jax.random.key(seed)
        ks = jax.random.split(key, 5)
        B, S = (2, 256)
        x = jax.random.normal(ks[0], (B, S, D_MODEL), dtype=jnp.float32)
        init = lambda k: jax.random.normal(k, (D_MODEL, D_MODEL), dtype=jnp.float32) * D_MODEL ** (-0.5)
        return {'x': x, 'Wq': init(ks[1]), 'Wk': init(ks[2]), 'Wv': init(ks[3]), 'Wo': init(ks[4])}
    _L0_attn_in = _L0_attn_setup()

    def _L0_ffn_setup():
        import jax, jax.numpy as jnp
        import numpy as np
        E, D, F = (8, 128, 512)
        B, S = (4, 256)

        def _layernorm(x, g, b, eps=1e-05):
            mu = jnp.mean(x, axis=-1, keepdims=True)
            var = jnp.var(x, axis=-1, keepdims=True)
            return (x - mu) * jax.lax.rsqrt(var + eps) * g + b
        key = jax.random.key(seed)
        ks = jax.random.split(key, 5)
        return {'input_features': jax.random.normal(ks[0], (B, S, D), jnp.float32), 'centroids': jax.random.normal(ks[1], (E, D), jnp.float32) * 0.1, 'ln_g': jnp.ones((E, D), jnp.float32), 'ln_b': jnp.zeros((E, D), jnp.float32), 'w1': jax.random.normal(ks[2], (E, F, D), jnp.float32) * (1.0 / np.sqrt(D).astype(np.float32)), 'b1': jnp.zeros((E, F), jnp.float32), 'w2': jax.random.normal(ks[3], (E, D, F), jnp.float32) * (1.0 / np.sqrt(F).astype(np.float32)), 'b2': jnp.zeros((E, D), jnp.float32)}
    _L0_ffn_in = _L0_ffn_setup()
    _d = {'L0_attn_x': _L0_attn_in['x'], 'L0_attn_Wq': _L0_attn_in['Wq'], 'L0_attn_Wk': _L0_attn_in['Wk'], 'L0_attn_Wv': _L0_attn_in['Wv'], 'L0_attn_Wo': _L0_attn_in['Wo'], 'L0_ffn_centroids': _L0_ffn_in['centroids'], 'L0_ffn_ln_g': _L0_ffn_in['ln_g'], 'L0_ffn_ln_b': _L0_ffn_in['ln_b'], 'L0_ffn_w1': _L0_ffn_in['w1'], 'L0_ffn_b1': _L0_ffn_in['b1'], 'L0_ffn_w2': _L0_ffn_in['w2'], 'L0_ffn_b2': _L0_ffn_in['b2']}
    _x0 = _d['L0_attn_x']
    _d['L0_attn_x'] = jax.random.normal(jax.random.fold_in(jax.random.key(seed), 1), (4, 512, 128), dtype=_x0.dtype)
    del _x0
    return _d

def reference(L0_attn_x, L0_attn_Wq, L0_attn_Wk, L0_attn_Wv, L0_attn_Wo, L0_ffn_centroids, L0_ffn_ln_g, L0_ffn_ln_b, L0_ffn_w1, L0_ffn_b1, L0_ffn_w2, L0_ffn_b2):

    def _L0_attn_ref(x, Wq, Wk, Wv, Wo):
        import jax, jax.numpy as jnp
        import numpy as np
        D_MODEL = 128
        NUM_HEADS = 16
        HEAD_DIM = D_MODEL // NUM_HEADS
        WINDOW = 128
        SCALE = HEAD_DIM ** (-0.5)
        B, S, _ = x.shape

        def heads(W):
            return (x @ W.T).reshape(B, S, NUM_HEADS, HEAD_DIM).transpose(0, 2, 1, 3)
        q, k, v = (heads(Wq), heads(Wk), heads(Wv))
        attn = jnp.einsum('bhqd,bhkd->bhqk', q, k) * SCALE
        idx = jnp.arange(S)
        band = jnp.abs(idx[:, None] - idx[None, :]) <= WINDOW
        attn = jnp.where(band[None, None], attn, -jnp.inf)
        attn = jax.nn.softmax(attn, axis=-1)
        out = jnp.einsum('bhqk,bhkd->bhqd', attn, v)
        out = out.transpose(0, 2, 1, 3).reshape(B, S, D_MODEL)
        return out @ Wo.T

    def _L0_ffn_ref(input_features, centroids, ln_g, ln_b, w1, b1, w2, b2):
        import jax, jax.numpy as jnp
        import numpy as np
        E, D, F = (8, 128, 512)
        B, S = (4, 256)

        def _layernorm(x, g, b, eps=1e-05):
            mu = jnp.mean(x, axis=-1, keepdims=True)
            var = jnp.var(x, axis=-1, keepdims=True)
            return (x - mu) * jax.lax.rsqrt(var + eps) * g + b
        Bf, Sf, Df = input_features.shape
        x = input_features.reshape(-1, Df)
        aff = x @ centroids.T
        assign = jnp.argmax(aff, axis=1)
        order = jnp.argsort(assign)
        xs = x[order]
        es = assign[order]
        alpha = jax.nn.sigmoid(jnp.take_along_axis(aff[order], es[:, None], axis=1))
        nE = centroids.shape[0]
        y = jnp.zeros_like(xs)
        for e in range(nE):
            h = _layernorm(xs, ln_g[e], ln_b[e])
            h = jax.nn.relu(h @ w1[e].T + b1[e])
            ye = xs + h @ w2[e].T + b2[e]
            y = y + jnp.where((es == e)[:, None], ye, 0.0)
        out_sorted = alpha * y + (1.0 - alpha) * xs
        inv = jnp.argsort(order)
        return out_sorted[inv].reshape(Bf, Sf, Df)
    x = L0_attn_x
    xn = _layernorm(x, axis=-1)
    s = _L0_attn_ref(xn, L0_attn_Wq, L0_attn_Wk, L0_attn_Wv, L0_attn_Wo)
    g = _silu(_L0_ffn_ref(xn, L0_ffn_centroids, L0_ffn_ln_g, L0_ffn_ln_b, L0_ffn_w1, L0_ffn_b1, L0_ffn_w2, L0_ffn_b2))
    x = x + s * g
    return x

_drawn_inputs = setup_inputs


def setup_inputs(seed=0):
    import zlib

    import numpy as np

    out = dict(_drawn_inputs(seed))
    spreads = {'L0_ffn_ln_g': (1.0, 0.6),
     'L0_ffn_ln_b': (0.0, 0.8),
     'L0_ffn_b1': (0.0, 0.8),
     'L0_ffn_b2': (0.0, 0.8)}
    factors = {}
    for name, (base, spread) in spreads.items():
        noise = np.random.default_rng([zlib.crc32(name.encode()), seed]).standard_normal(out[name].shape)
        drawn = base * np.exp(spread * noise) if base else spread * noise
        out[name] = jnp.asarray(drawn.astype(out[name].dtype))
    for name, factor in factors.items():
        out[name] = (out[name] * factor).astype(out[name].dtype)
    return out
```

```python
from contextlib import ExitStack

import concourse.bass as bass
from concourse import mybir

ALU = mybir.AluOpType
ACT = mybir.ActivationFunctionType
AX = mybir.AxisListType
F32 = mybir.dt.float32
F32R = mybir.dt.float32r
BF16 = mybir.dt.bfloat16
I32 = mybir.dt.int32
U32 = mybir.dt.uint32

P = 128


def build(nc, x, wq_t, wk_t, wv_t, wo_t, cent_t, ln_g_t, ln_b_t, w1_t, b1_t, w2_t, b2, ident_in, out):
    T, D = x.shape
    B = 4
    S = T // B
    NT = T // P
    QT = S // P
    DH = 8
    H = D // DH
    G = H // 4
    SCALE = DH ** -0.5
    E = cent_t.shape[1]
    F = w1_t.shape[2]
    FC = F // P
    EPS = 1e-5
    NS = (T - E) // P + E
    ROW = D + 1
    UNITS = B * G
    STEPS = UNITS * QT
    LAG = 2
    RING = 3
    VW = DH + 1
    BASE0 = QT * 2
    FFN_AT = STEPS // 2
    W1W, B1W, W2W = F, FC, FC * D
    O_B1, O_W2, O_B2 = W1W, W1W + B1W, W1W + B1W + W2W
    WW = O_B2 + D
    ST1 = W1W + B1W
    ST2 = W2W + D

    def q_tiles(kt):
        return max(0, kt - 1), min(QT, kt + 2)

    tasks = []
    for t in range(-1, STEPS + 8):
        u, kt = divmod(t, QT)
        g, b = u % G, u // G
        if t == -1:
            tasks += [(t, "max_t", 0), (t, "max_t", 1)]
            continue
        if t == 0:
            tasks.append((t, "affinity", 0))
        if t == 2:
            tasks.append((t, "prefix", 0))
        if t == 5:
            tasks.append((t, "bias1", 0))
        if kt == 0 and 1 <= u and u + 1 < UNITS:
            tasks.append((t, "max_t", u + 1))
        if kt == 1 and g == 0 and b + 1 < B:
            tasks.append((t, "q_proj", b + 1))
        if kt == 3 and g == 0 and b + 1 < B:
            tasks.append((t, "k_proj", b + 1))
        if kt == 2 and 1 <= u <= UNITS:
            tasks.append((t, "o_turn", u - 1))
        if kt == 1 and g == 1 and b >= 1:
            tasks.append((t, "on_turn", b - 1))
        if kt == 3 and g == 1 and b >= 1:
            tasks.append((t, "wo", b - 1))
    TURNS = (NS + 3) // 4
    assert TURNS == 6 and len({t for t, _, _ in tasks if t >= 0}) == len(tasks) - 2
    number = {(kind, arg): m for m, (_, kind, arg) in enumerate(tasks)}
    END = max(t for t, _, _ in tasks) + 1

    def tasks_at(t):
        return [(kind, arg) for at, kind, arg in tasks if at == t]

    with ExitStack() as ctx:
        def sb(name, shape, dt=F32):
            return ctx.enter_context(nc.sbuf_tensor(name, shape, dt)).ap()

        def sem(name):
            return ctx.enter_context(nc.semaphore(name))

        ident = sb("ident", [P, P])
        before = sb("before", [P, P], BF16)
        ones_b = sb("ones_b", [P, P], BF16)
        xn = sb("xn", [P, NT, D])
        zrow = sb("zrow", [P, NT, ROW])
        xnT = sb("xnT", [P, T])
        wqk = sb("wqk", [P, 4, D])
        cent = sb("cent", [P, E])
        lng = sb("lng", [P, E])
        lnb = sb("lnb", [P, E])
        wall = sb("wall", [P, E, WW])
        wall_flat = wall.rearrange("p e w -> p (e w)")
        vp = sb("vp", [P, NT * H * VW + 32 - VW])
        qhl = sb("qhl", [P, 2, S], F32R)
        khl = sb("khl", [P, 2, S], F32R)
        qst = sb("qst", [P, 4, 4, S], F32R)
        kst = sb("kst", [P, 2, G, S], F32R)
        mneg = sb("mneg", [P, 2, 4 * QT])
        mT = sb("mT", [4 * QT, 2, P], F32R)
        probs = sb("probs", [P, RING, 4, 3 * P])
        oT = sb("oT", [P, 2, S])
        rden = sb("rden", [P, 2, QT, 4])
        on = sb("on", [P, QT, D])
        onT = sb("onT", [P, S])
        s_all = sb("s_all", [P, NT, D])
        gtmp = sb("gtmp", [P, 2, QT * D])
        stats = sb("stats", [P, NT, 6])
        mv = sb("mv", [P, NT, 2])
        vare = sb("vare", [P, NT])
        rstd = sb("rstd", [P, NT])
        stats2 = sb("stats2", [P, NT, 6])
        mv2 = sb("mv2", [P, NT, 2])
        vare2 = sb("vare2", [P, NT])
        rstd2 = sb("rstd2", [P, NT])
        mhalf = sb("mhalf", [P, NT])
        pool_ws = sb("pool_ws", [P, 2 * ST1 + 2 * ST2 + 2 * F])
        zs = pool_ws[:, 0:NS * ROW].rearrange("p (j r) -> p j r", r=ROW)
        o = 0
        stage1, stage2, hid = [], [], []
        for par in range(2):
            stage1.append(pool_ws[:, o:o + ST1])
            o += ST1
        for par in range(2):
            stage2.append(pool_ws[:, o:o + ST2])
            o += ST2
        for par in range(2):
            hid.append(pool_ws[:, o:o + F])
            o += F
        zT = sb("zT", [P, NS * P])
        dest = sb("dest", [P, NS], I32)
        dest1 = sb("dest1", [P, 2, 1], I32)
        ysb = sb("ysb", [P, 2, D])
        aff = sb("aff", [P, NT, E])
        amax = sb("amax", [P, NT])
        alpha = sb("alpha", [P, NT])
        ea = sb("ea", [P, NT])
        iseq = sb("iseq", [P, NT, E])
        firstw = sb("firstw", [P, E])
        fmax = sb("fmax", [P, NT])
        oneh = sb("oneh", [P, E, NT])
        rowtot = sb("rowtot", [P, E], BF16)
        oneF = sb("oneF", [P, E * NT])
        scan = sb("scan", [P, E, NT])
        pre = sb("pre", [P, 2 * E])
        npad_f = sb("npad_f", [P, E])
        npad_i = sb("npad_i", [P, E], I32)
        npad_j = sb("npad_j", [P, E], I32)
        npad = sb("npad", [P, E])
        ends = sb("ends", [P, E])
        offs = sb("offs", [P, E])
        offs2 = sb("offs2", [P, E])
        slotw = sb("slotw", [P, E, NT])
        slotv = sb("slotv", [P, E, NT])
        slotf = sb("slotf", [P, NT])
        slot = sb("slot", [P, NT], I32)
        starts = sb("starts", [1, NS + 1, E])
        below = sb("below", [1, NS + 1, E])
        expf = sb("expf", [1, NS + 1])
        expert = sb("expert", [1, NS + 1], I32)
        ps = ctx.enter_context(nc.psum_tensor("ps", [P, 8, 512], F32))
        ST, SM, PV, MISC = 0, 2, 6, 7

        z_dram = nc.dram_tensor("z_dram", (NS * P, ROW), F32, kind="Internal").ap()
        f_dram = nc.dram_tensor("f_dram", (T + NS * P, D), F32, kind="Internal").ap()

        x_in = [sem(f"x_in{b}") for b in range(B)]
        ident_in_s = sem("ident_in_s")
        proj_in = sem("proj_in")
        small_in = sem("small_in")
        w_in = sem("w_in")
        consts_set = sem("consts_set")
        vp_set = sem("vp_set")
        qst_zero = sem("qst_zero")
        kst_ones = sem("kst_ones")
        var_done = sem("var_done")
        rstd_done = sem("rstd_done")
        xn_done = sem("xn_done")
        stat_step = sem("stat_step")
        xnT_full = sem("xnT_full")
        xnT_done = sem("xnT_done")
        v_full = sem("v_full")
        v_done = sem("v_done")
        qk0_full = sem("qk0_full")
        hi_done = sem("hi_done")
        lo_done = sem("lo_done")
        q_placed = [sem(f"q_placed{r}") for r in range(4)]
        k_placed = [sem(f"k_placed{r}") for r in range(2)]
        s_full = sem("s_full")
        s_max = sem("s_max")
        m_turned = sem("m_turned")
        m_placed = [sem(f"m_placed{r}") for r in range(4)]
        st_full = sem("st_full")
        exp_done = sem("exp_done")
        p_masked = sem("p_masked")
        pv_done = sem("pv_done")
        pv_copied = sem("pv_copied")
        misc_full = sem("misc_full")
        misc_empty = sem("misc_empty")
        rden_done = sem("rden_done")
        o_normed = sem("o_normed")
        on_turned = sem("on_turned")
        s_ready = sem("s_ready")
        aff_done = sem("aff_done")
        amax_done = sem("amax_done")
        ea_done = sem("ea_done")
        alpha_done = sem("alpha_done")
        route = sem("route")
        rowtot_done = sem("rowtot_done")
        slots_done = sem("slots_done")
        experts_done = sem("experts_done")
        pre_made = sem("pre_made")
        z_cleared = sem("z_cleared")
        var2_done = sem("var2_done")
        rstd2_done = sem("rstd2_done")
        z_done = sem("z_done")
        z_sent = sem("z_sent")
        zs_in = sem("zs_in")
        dest_copied = sem("dest_copied")
        z_turned = sem("z_turned")
        zT_dve = sem("zT_dve")
        zT_act = sem("zT_act")
        b1_done = sem("b1_done")
        w1_folded = sem("w1_folded")
        w1_staged = sem("w1_staged")
        w2_staged = sem("w2_staged")
        dest_staged = sem("dest_staged")
        sending = sem("sending")
        h_full = sem("h_full")
        h_dve = sem("h_dve")
        h_act = sem("h_act")
        y_full = sem("y_full")
        y_copied = sem("y_copied")
        y_sent = [sem(f"y_sent{r}") for r in range(2)]
        f_in = [sem(f"f_in{b}") for b in range(B)]
        x_again = [sem(f"x_again{b}") for b in range(B)]
        gate_in = sem("gate_in")
        gate_exp = sem("gate_exp")
        gate_plus = sem("gate_plus")
        gate_rec = sem("gate_rec")
        gate_done = sem("gate_done")
        pool_step = sem("pool_step")
        res_done = sem("res_done")
        stored = sem("stored")

        def bank(n):
            return ps[:, n, :]

        def gate_at(b):
            return FFN_AT + 3 + 4 * b

        def raw(ap):
            return ap.bitcast(F32)

        def lhs_v(tile, h):
            o = (tile * H + h) * VW
            return vp[:, o:o + 32]

        def s_width(qt):
            lo, hi = q_tiles(qt)
            return (hi - lo) * P

        x_tok = x.rearrange("(c p) d -> p c d", p=P)
        out_tok = out.rearrange("(c p) d -> p c d", p=P)
        f_tok = f_dram[0:T, :].rearrange("(c p) d -> p c d", p=P)

        block = ctx.enter_context(nc.Block())

        @block.sync
        def _(sp):
            def load_x(b):
                sp.dma_start(xn[:, QT * b:QT * (b + 1), :], x_tok[:, QT * b:QT * (b + 1), :]).then_inc(x_in[b], 16)

            load_x(0)
            sp.dma_start(ident[:], ident_in).then_inc(ident_in_s, 16)
            for n, w in enumerate((wq_t, wk_t, wv_t, wo_t)):
                sp.dma_start(wqk[:, n, :], w).then_inc(proj_in, 16)
            for b in range(1, B):
                load_x(b)
            sp.dma_start(cent[:], cent_t).then_inc(small_in, 16)
            sp.dma_start(lng[:], ln_g_t).then_inc(small_in, 16)
            sp.dma_start(lnb[:], ln_b_t).then_inc(small_in, 16)

            def place_q(u):
                b, g, r = u // G, u % G, u % 4
                sp.wait_ge(lo_done, 2 * b + 1)
                if u == 0:
                    sp.wait_ge(qst_zero, 1)
                if u >= 4:
                    sp.wait_ge(st_full, 16 * (u - 3))
                for slot_n, part in enumerate((0, 0, 1)):
                    for j in range(4):
                        sp.dma_start(raw(qst[32 * slot_n + 8 * j:32 * slot_n + 8 * j + 8, r, j, :]),
                                     raw(qhl[32 * g + 8 * j:32 * g + 8 * j + 8, part, :])).then_inc(q_placed[r], 16)

            def place_k(b):
                sp.wait_ge(lo_done, 2 * b + 2)
                if b >= 2:
                    sp.wait_ge(st_full, 16 * G * (b - 1))
                for slot_n, part in enumerate((0, 1, 0)):
                    for g in range(G):
                        sp.dma_start(raw(kst[32 * slot_n:32 * slot_n + 32, b % 2, g, :]),
                                     raw(khl[32 * g:32 * g + 32, part, :])).then_inc(k_placed[b % 2], 16)

            def place_m(u):
                sp.wait_ge(m_turned, u + 1)
                if u >= 4:
                    sp.wait_ge(st_full, 16 * (u - 3))
                for j in range(4):
                    sp.dma_start(raw(qst[96 + 8 * j:97 + 8 * j, u % 4, j, :]),
                                 raw(mT[QT * j:QT * (j + 1), u % 2, :])).then_inc(m_placed[u % 4], 16)

            place_q(0)
            place_k(0)
            place_q(1)
            for e in range(E):
                sp.dma_start(wall[:, e, 0:O_B1], w1_t[:, e, :]).then_inc(w_in, 16)
                sp.dma_start(wall[:, e, O_B1:O_W2], b1_t[:, e, :]).then_inc(w_in, 16)
                sp.dma_start(wall[:, e, O_W2:O_B2], w2_t[:, e, :]).then_inc(w_in, 16)
                sp.dma_start(wall[:, e, O_B2:WW], b2[e:e + 1, :].broadcast_to([P, D])).then_inc(w_in, 16)
            place_q(2)
            place_q(3)
            sp.wait_ge(pre_made, 2)
            sp.dma_start(z_dram.rearrange("(j p) r -> p j r", p=P), zs).then_inc(z_cleared, 16)
            place_m(0)
            place_m(1)
            for u in range(UNITS):
                if u >= 1 and u + 3 < UNITS:
                    if (u + 3) % G == 0:
                        place_k((u + 3) // G)
                    place_q(u + 3)
                if u + 2 < UNITS:
                    place_m(u + 2)
                if u == 4:
                    sp.wait_ge(z_sent, 16 * NT)
                    sp.dma_start(zs, z_dram.rearrange("(j p) r -> p j r", p=P)).then_inc(zs_in, 16)
                if u == FFN_AT // QT - 1:
                    sp.wait_ge(y_sent[0], 16 * ((NS + 1) // 2))
                    sp.wait_ge(y_sent[1], 16 * (NS // 2))
                    for c in range(B):
                        sp.dma_start(zrow[:, QT * c:QT * (c + 1), 0:D], f_tok[:, QT * c:QT * (c + 1), :]
                                     ).then_inc(f_in[c], 16)
            for b in range(B):
                sp.wait_ge(res_done, b + 1)
                sp.dma_start(out_tok[:, QT * b:QT * (b + 1), :], s_all[:, QT * b:QT * (b + 1), :]
                             ).then_inc(stored, 16)
            sp.wait_ge(stored, 16 * B)

        @block.tensor
        def _(pe):
            def turn_x(b):
                pe.wait_ge(xn_done, b + 1)
                for c in range(QT):
                    mm = nc.tensor.transpose(ps[:, b, P * c:P * (c + 1)], xn[:, QT * b + c, :], ident[:])
                mm.then_inc(xnT_full, 1)

            def project(dst, w, b):
                return nc.tensor.matmul(dst, wqk[:, w, :], xnT[:, S * b:S * (b + 1)], start=True, stop=True)

            def values(b):
                pe.wait_ge(xnT_done, b + 1)
                if b >= 2:
                    pe.wait_ge(v_done, b - 1)
                for c in range(QT):
                    mm = nc.tensor.matmul(ps[:, 6 + b % 2, P * c:P * (c + 1)],
                                          xnT[:, S * b + P * c:S * b + P * (c + 1)], wqk[:, 2, :],
                                          start=True, stop=True)
                mm.then_inc(v_full, 1)

            def maxima_item(n):
                u, rest = divmod(n, 2 * QT)
                qt, jj = divmod(rest, 2)
                b, g, r = u // G, u % G, u % 4
                lo, hi = q_tiles(qt)
                if rest == 0:
                    pe.wait_ge(q_placed[r], 16 * 12 * (u // 4 + 1))
                    pe.wait_ge(k_placed[b % 2], 16 * 12 * (b // 2 + 1))
                if n >= 2:
                    pe.wait_ge(s_max, n - 1)
                for i in range(2):
                    mm = nc.tensor.matmul(ps[:, SM + 2 * (n % 2) + i, 0:P * (hi - lo)],
                                          qst[0:96, r, 2 * jj + i, P * qt:P * (qt + 1)],
                                          kst[0:96, b % 2, g, P * lo:P * hi], start=True, stop=True)
                mm.then_inc(s_full, 1)

            def score(t, j):
                u, kt = divmod(t, QT)
                b, g = u // G, u % G
                n = 4 * t + j
                lo, hi = q_tiles(kt)
                if kt == 0 and j == 0:
                    pe.wait_ge(m_placed[u % 4], 64 * (u // 4 + 1))
                if n >= 2:
                    pe.wait_ge(exp_done, n - 1)
                nc.tensor.matmul(ps[:, ST + n % 2, 0:P * (hi - lo)], kst[:, b % 2, g, P * kt:P * (kt + 1)],
                                 qst[:, u % 4, j, P * lo:P * hi], start=True, stop=True).then_inc(st_full, 1)

            def weighted(t):
                u, kt = divmod(t, QT)
                b, g = u // G, u % G
                lo, hi = q_tiles(kt)
                pe.wait_ge(p_masked, t + 1)
                if kt == 0 and u >= 1:
                    pe.wait_ge(pv_copied, u)
                for j in range(4):
                    mm = nc.tensor.matmul(ps[32 * j:32 * j + 32, PV, P * lo:P * hi],
                                          lhs_v(QT * b + kt, 4 * g + j), probs[:, t % RING, j, 0:P * (hi - lo)],
                                          start=(kt == 0), stop=(kt == QT - 1), skip_group_check=True)
                mm.then_inc(pv_done, 1)

            def task(kind, arg):
                m = number[kind, arg]
                if m >= 1:
                    pe.wait_ge(misc_empty, m)
                dst = bank(MISC)
                if kind == "max_t":
                    pe.wait_ge(s_max, 2 * QT * (arg + 1))
                    mm = nc.tensor.transpose(dst[0:4 * QT, 0:P], mneg[:, arg % 2, :], ident[:])
                elif kind == "affinity":
                    pe.wait_ge(small_in, 48)
                    for c in range(NT):
                        mm = nc.tensor.matmul(dst[:, E * c:E * (c + 1)], xnT[:, P * c:P * (c + 1)], cent[:],
                                              start=True, stop=True)
                elif kind == "prefix":
                    pe.wait_ge(rowtot_done, 1)
                    pe.wait_ge(consts_set, 6)
                    nc.tensor.matmul(dst[:, 0:E], before[:], rowtot[:], start=True, stop=True)
                    mm = nc.tensor.matmul(dst[:, E:2 * E], ones_b[:], rowtot[:], start=True, stop=True)
                elif kind == "bias1":
                    pe.wait_ge(w_in, 16 * 4 * E)
                    for e in range(E):
                        for c in range(FC):
                            mm = nc.tensor.matmul(dst[:, FC * e + c:FC * e + c + 1],
                                                  wall[:, e, P * c:P * (c + 1)], lnb[:, e:e + 1],
                                                  start=True, stop=True)
                elif kind == "q_proj":
                    mm = project(dst, 0, arg)
                elif kind == "k_proj":
                    mm = project(dst, 1, arg)
                elif kind == "o_turn":
                    pe.wait_ge(pv_copied, arg + 1)
                    for qt in range(QT):
                        mm = nc.tensor.transpose(dst[:, P * qt:P * (qt + 1)], oT[:, arg % 2, P * qt:P * (qt + 1)],
                                                 ident[:])
                elif kind == "on_turn":
                    pe.wait_ge(o_normed, G * (arg + 1))
                    for qt in range(QT):
                        mm = nc.tensor.transpose(dst[:, P * qt:P * (qt + 1)], on[:, qt, :], ident[:])
                elif kind == "wo":
                    pe.wait_ge(on_turned, arg + 1)
                    for qt in range(QT):
                        mm = nc.tensor.matmul(dst[:, P * qt:P * (qt + 1)], onT[:, P * qt:P * (qt + 1)], wqk[:, 3, :],
                                              start=True, stop=True)
                mm.then_inc(misc_full, 1)

            def hidden(j, par):
                pe.wait_ge(w1_staged, j + 1)
                if not isinstance(j, int) or j >= 2:
                    pe.wait_ge(h_dve, j - 1)
                    pe.wait_ge(h_act, j - 1)
                for c in range(FC):
                    mm = nc.tensor.matmul(ps[:, 2 * par + c // 2, P * (c % 2):P * (c % 2) + P],
                                          stage1[par][:, P * c:P * (c + 1)], zT[:, bass.ds(j * P, P)],
                                          start=True, stop=True)
                mm.then_inc(h_full, 1)

            def output(j, par):
                pe.wait_ge(w2_staged, j + 1)
                pe.wait_ge(h_dve, j + 1)
                pe.wait_ge(h_act, j + 1)
                if not isinstance(j, int) or j >= 2:
                    pe.wait_ge(y_copied, j - 1)
                for c in range(FC):
                    mm = nc.tensor.matmul(ps[:, 4 + par, 0:P], hid[par][:, P * c:P * (c + 1)],
                                          stage2[par][:, P * c:P * (c + 1)], start=(c == 0), stop=(c == FC - 1))
                mm.then_inc(y_full, 1)

            def feed_forward():
                pe.wait_ge(exp_done, 4 * FFN_AT)
                pe.wait_ge(s_max, BASE0 * (FFN_AT // QT + 2))
                pe.wait_ge(zs_in, 16)
                for n in range(TURNS):
                    for c in range(4 * n, min(4 * n + 4, NS)):
                        mm = nc.tensor.transpose(ps[:, n, P * (c % 4):P * (c % 4) + P], zs[:, c, 0:D], ident[:])
                    mm.then_inc(z_turned, 1)
                pe.wait_ge(zT_dve, TURNS // 2)
                pe.wait_ge(zT_act, TURNS // 2)
                hidden(0, 0)
                hidden(1, 1)
                output(0, 0)
                hidden(2, 0)
                output(1, 1)
                with pe.Fori(1, NS // 2) as i:
                    hidden(2 * i + 1, 1)
                    output(2 * i, 0)
                    hidden(2 * i + 2, 0)
                    output(2 * i + 1, 1)
                output(NS - 1, (NS - 1) % 2)
                pe.wait_ge(y_copied, NS)

            pe.wait_ge(ident_in_s, 16)
            turn_x(0)
            pe.wait_ge(xnT_done, 1)
            pe.wait_ge(proj_in, 64)
            project(bank(4), 0, 0).then_inc(qk0_full, 1)
            project(bank(5), 1, 0).then_inc(qk0_full, 1)
            values(0)
            for b in range(1, B):
                turn_x(b)
                values(b)
            pe.wait_ge(xnT_done, B)
            pe.wait_ge(lo_done, 2)
            pe.wait_ge(v_done, B)
            for n in range(2 * BASE0):
                maxima_item(n)
            for kind, arg in tasks_at(-1):
                task(kind, arg)
            for t in range(END):
                if t == FFN_AT:
                    feed_forward()
                more = t < STEPS - 2 * QT
                if t < STEPS:
                    score(t, 0)
                    score(t, 1)
                    if more:
                        maxima_item(2 * BASE0 + 2 * t)
                    score(t, 2)
                    if more:
                        maxima_item(2 * BASE0 + 2 * t + 1)
                    score(t, 3)
                if LAG <= t < STEPS + LAG:
                    weighted(t - LAG)
                for kind, arg in tasks_at(t):
                    task(kind, arg)

        @block.vector
        def _(dve):
            steps = [0]

            def link(ins):
                steps[0] += 1
                ins.then_inc(route, 1)
                dve.wait_ge(route, steps[0])

            def moments(b, src, st, m):
                for c in range(QT * b, QT * (b + 1)):
                    nc.vector.bn_stats(st[:, c, :], src[:, c, 0:D]).then_inc(stat_step, 1)
                dve.wait_ge(stat_step, stat_count(QT))
                for c in range(QT * b, QT * (b + 1)):
                    last = nc.vector.bn_aggr(m[:, c, :], st[:, c, :])
                return last

            counted = [0]

            def stat_count(n):
                counted[0] += n
                return counted[0]

            def norm(b):
                dve.wait_ge(rstd_done, b + 1)
                for c in range(QT * b, QT * (b + 1)):
                    last = nc.vector.tensor_scalar(xn[:, c, :], xn[:, c, :], mv[:, c, 0:1], rstd[:, c:c + 1],
                                                   ALU.subtract, ALU.mult)
                last.then_inc(xn_done, 1)

            def copy_xT(b):
                dve.wait_ge(xnT_full, b + 1)
                nc.vector.tensor_copy(xnT[:, S * b:S * (b + 1)], bank(b)).then_inc(xnT_done, 1)

            def low_part(b, which, src):
                dve.wait_ge(hi_done, 2 * b + which + 1)
                hl = (qhl, khl)[which]
                return nc.vector.tensor_tensor(hl[:, 1, :], src, hl[:, 0, :].bitcast(F32), ALU.subtract)

            def maxima(n):
                u, rest = divmod(n, 2 * QT)
                qt, jj = divmod(rest, 2)
                dve.wait_ge(s_full, n + 1)
                if rest == 0 and u >= 2:
                    dve.wait_ge(misc_full, number["max_t", u - 2] + 1)
                dst = mneg[:, u % 2, :].rearrange("p (j q) -> p j q", q=QT)[:, 2 * jj:2 * jj + 2, qt]
                a = SM + 2 * (n % 2)
                nc.vector.tensor_reduce(dst, ps[:, a:a + 2, 0:s_width(qt)], AX.X, ALU.max,
                                        negate=True).then_inc(s_max, 1)

            def copy_pv(u):
                dve.wait_ge(pv_done, QT * (u + 1))
                nc.vector.tensor_copy(oT[:, u % 2, :], bank(PV)).then_inc(pv_copied, 1)

            def task(kind, arg):
                m = number[kind, arg]
                if kind in ("on_turn", "wo"):
                    return
                dve.wait_ge(misc_full, m + 1)
                src = bank(MISC)
                if kind == "max_t":
                    if arg >= 2:
                        dve.wait_ge(m_placed[(arg - 2) % 4], 64 * ((arg - 2) // 4 + 1))
                    nc.vector.tensor_copy(mT[:, arg % 2, :], src[0:4 * QT, 0:P]).then_inc(m_turned, 1)
                    dve.wait_ge(m_turned, arg + 1)
                    dve.sem_inc(misc_empty, 1)
                elif kind == "affinity":
                    nc.vector.tensor_copy(aff.rearrange("p c e -> p (c e)"), src[:, 0:NT * E]).then_inc(misc_empty, 1)
                    dve.wait_ge(misc_empty, m + 1)
                    link(nc.vector.tensor_reduce(amax[:], aff[:], AX.X, ALU.max))
                    nc.vector.engine_nop().then_inc(amax_done, 1)
                    link(nc.vector.tensor_tensor(iseq[:], aff[:], amax.unsqueeze(2).broadcast_to([P, NT, E]), ALU.is_equal))
                    dve.wait_ge(consts_set, 6)
                    link(nc.vector.tensor_tensor(iseq[:], iseq[:], firstw.unsqueeze(1).broadcast_to([P, NT, E]), ALU.mult))
                    link(nc.vector.tensor_reduce(fmax[:], iseq[:], AX.X, ALU.max))
                    link(nc.vector.tensor_tensor(oneh.rearrange("p e c -> p c e"), iseq[:],
                                                 fmax.unsqueeze(2).broadcast_to([P, NT, E]), ALU.is_equal))
                    nc.vector.tensor_reduce(npad_f[:], oneh[:], AX.X, ALU.add).then_inc(route, 1)
                    steps[0] += 1
                    dve.wait_ge(route, steps[0])
                    nc.vector.tensor_copy(rowtot[:], npad_f[:]).then_inc(rowtot_done, 1)
                    link(nc.vector.tensor_tensor_scan(scan.rearrange("p e c -> p (e c)"), oneF[:],
                                                      oneh.rearrange("p e c -> p (e c)"), 0.0, ALU.mult, ALU.add))
                elif kind == "prefix":
                    nc.vector.tensor_copy(pre[:], src[:, 0:2 * E]).then_inc(misc_empty, 1)
                    dve.wait_ge(misc_empty, m + 1)
                    link(nc.vector.tensor_scalar(npad_i[:], pre[:, E:2 * E], float(P - 1), None, ALU.add))
                    link(nc.vector.tensor_scalar(npad_j[:], npad_i[:], 7, 7, ALU.logical_shift_right,
                                                 ALU.logical_shift_left))
                    link(nc.vector.tensor_copy(npad[:], npad_j[:]))
                    link(nc.vector.tensor_tensor_scan(ends[:], oneF[:, 0:E], npad[:], 0.0, ALU.mult, ALU.add))
                    link(nc.vector.tensor_tensor(offs[:], ends[:], npad[:], ALU.subtract))
                    link(nc.vector.tensor_tensor(offs2[:], offs[:], pre[:, 0:E], ALU.add))
                    link(nc.vector.tensor_tensor(offs2[:, 1:E], offs2[:, 1:E], scan[:, 0:E - 1, NT - 1], ALU.subtract))
                    link(nc.vector.tensor_tensor(slotw[:], scan[:], offs2.unsqueeze(2).broadcast_to([P, E, NT]), ALU.add))
                    link(nc.vector.tensor_tensor(slotv[:], slotw[:], oneh[:], ALU.mult))
                    link(nc.vector.tensor_reduce(slotf[:], slotv.rearrange("p e c -> p c e"), AX.X, ALU.add))
                    nc.vector.tensor_scalar(slot[:], slotf[:], -1.0, None, ALU.add).then_inc(slots_done, 1)
                    link(nc.vector.tensor_tensor(below[:], starts[:], ends[0:1, :].unsqueeze(1).broadcast_to([1, NS + 1, E]),
                                                 ALU.is_ge))
                    link(nc.vector.tensor_reduce(expf[:], below[:], AX.X, ALU.add))
                    nc.vector.tensor_scalar(expert[:], expf[:], float(E - 1), None, ALU.min).then_inc(experts_done, 1)
                    dve.wait_ge(ea_done, 1)
                    link(nc.vector.tensor_scalar(ea[:], ea[:], 1.0, None, ALU.add))
                    nc.vector.reciprocal(alpha[:], ea[:]).then_inc(alpha_done, 1)
                elif kind == "bias1":
                    wb = wall[:, :, O_B1:O_W2]
                    nc.vector.tensor_tensor(wb, wb, src[:, 0:E * FC].rearrange("p (e c) -> p e c", c=FC),
                                            ALU.add).then_inc(b1_done, 1)
                    dve.wait_ge(b1_done, 1)
                    dve.sem_inc(misc_empty, 1)
                elif kind in ("q_proj", "k_proj"):
                    which = 0 if kind == "q_proj" else 1
                    low_part(arg, which, src).then_inc(lo_done, 1)
                    dve.wait_ge(lo_done, 2 * arg + which + 1)
                    dve.sem_inc(misc_empty, 1)
                elif kind == "o_turn":
                    b, g = arg // G, arg % G
                    t4 = src.rearrange("p (q j w) -> p q j w", j=4, w=32)
                    nc.vector.reciprocal(rden[:, arg % 2, :, :], t4[:, :, :, DH]).then_inc(rden_done, 1)
                    dve.wait_ge(rden_done, arg + 1)
                    if g == 0 and b >= 1:
                        dve.wait_ge(misc_full, number["on_turn", b - 1] + 1)
                    dst = on[:, :, 32 * g:32 * g + 32].rearrange("p q (j d) -> p q j d", d=DH)
                    nc.vector.tensor_tensor(dst, t4[:, :, :, 0:DH],
                                            rden[:, arg % 2, :, :].unsqueeze(3).broadcast_to([P, QT, 4, DH]),
                                            ALU.mult).then_inc(o_normed, 1)
                    dve.wait_ge(o_normed, arg + 1)
                    dve.sem_inc(misc_empty, 1)

            def relu_half(j, par):
                dve.wait_ge(h_full, j + 1)
                for c in range(FC // 2):
                    last = nc.vector.tensor_scalar(hid[par][:, P * c:P * (c + 1)], ps[:, 2 * par, P * c:P * (c + 1)],
                                                   stage1[par][:, F + c:F + c + 1], 0.0, ALU.add, ALU.max)
                last.then_inc(h_dve, 1)

            def copy_y(j, par):
                dve.wait_ge(y_full, j + 1)
                if not isinstance(j, int):
                    dve.wait_ge(y_sent[par], 8 * (j - par))
                elif j >= 2:
                    dve.wait_ge(y_sent[par], 16 * (j // 2))
                nc.vector.tensor_tensor(ysb[:, par, :], ps[:, 4 + par, 0:P], stage2[par][:, W2W:W2W + D],
                                        ALU.add).then_inc(y_copied, 1)

            def feed_forward():
                for n in range(0, TURNS, 2):
                    dve.wait_ge(z_turned, n + 1)
                    w = P * (min(4 * n + 4, NS) - 4 * n)
                    nc.vector.tensor_copy(zT[:, 4 * P * n:4 * P * n + w], ps[:, n, 0:w]).then_inc(zT_dve, 1)
                relu_half(0, 0)
                relu_half(1, 1)
                copy_y(0, 0)
                relu_half(2, 0)
                copy_y(1, 1)
                with dve.Fori(1, NS // 2) as i:
                    relu_half(2 * i + 1, 1)
                    copy_y(2 * i, 0)
                    relu_half(2 * i + 2, 0)
                    copy_y(2 * i + 1, 1)
                copy_y(NS - 1, (NS - 1) % 2)

            nc.vector.memset(oneF[:], 1.0).then_inc(consts_set, 1)
            nc.vector.memset(ones_b[:], 1.0).then_inc(consts_set, 1)
            nc.vector.memset(vp[:], 1.0).then_inc(vp_set, 1)
            for b in range(B):
                dve.wait_ge(x_in[b], 16)
                moments(b, xn, stats, mv).then_inc(var_done, 1)
                if b == 0:
                    norm(0)
                    copy_xT(0)
                    low_part(0, 0, bank(4)).then_inc(lo_done, 1)
                    low_part(0, 1, bank(5)).then_inc(lo_done, 1)
            for b in range(1, B):
                norm(b)
                copy_xT(b)
            for n in range(2 * BASE0):
                maxima(n)
            for kind, arg in tasks_at(-1):
                task(kind, arg)
            for t in range(END + 1):
                if t == FFN_AT:
                    feed_forward()
                more = t < STEPS - 2 * QT
                if more:
                    maxima(2 * BASE0 + 2 * t)
                u, kt = divmod(t, QT)
                if kt == 2 and 1 <= u <= UNITS:
                    copy_pv(u - 1)
                if t >= 1:
                    for kind, arg in tasks_at(t - 1):
                        task(kind, arg)
                if more:
                    maxima(2 * BASE0 + 2 * t + 1)
                if 2 <= t < 2 + B:
                    moments(t - 2, xn, stats2, mv2).then_inc(var2_done, 1)
                for b in range(B):
                    if t == gate_at(b) + 1:
                        dve.wait_ge(gate_plus, b + 1)
                        nc.vector.reciprocal(gtmp[:, b % 2, :], gtmp[:, b % 2, :]).then_inc(gate_rec, 1)

        @block.scalar
        def _(act):
            def values(b):
                act.wait_ge(v_full, b + 1)
                if b == 0:
                    act.wait_ge(vp_set, 1)
                o = QT * b * H * VW
                dst = vp[:, o:o + QT * H * VW].rearrange("p (c h w) -> p c h w", h=H, w=VW)
                src = ps[:, 6 + b % 2, :].rearrange("p (c h w) -> p c h w", h=H, w=DH)
                for c in range(QT):
                    last = nc.scalar.activation(dst[:, c, :, 0:DH], src[:, c, :, :], ACT.Copy)
                last.then_inc(v_done, 1)

            def high_part(b, which, src):
                if b >= 1 and which == 0:
                    for r in range(4):
                        act.wait_ge(q_placed[r], 16 * 12 * b)
                if b >= 1 and which == 1:
                    act.wait_ge(k_placed[(b - 1) % 2], 16 * 12 * ((b - 1) // 2 + 1))
                nc.scalar.activation((qhl, khl)[which][:, 0, :], src, ACT.Copy).then_inc(hi_done, 1)

            def exponentials(t, j):
                u, kt = divmod(t, QT)
                lo, hi = q_tiles(kt)
                n = 4 * t + j
                act.wait_ge(st_full, n + 1)
                if j == 0 and t >= RING:
                    act.wait_ge(pv_done, t - RING + 1)
                nc.scalar.activation(probs[:, t % RING, j, 0:P * (hi - lo)], ps[:, ST + n % 2, 0:P * (hi - lo)],
                                     ACT.Exp, scale=SCALE).then_inc(exp_done, 1)

            def task(kind, arg):
                m = number[kind, arg]
                src = bank(MISC)
                if kind in ("q_proj", "k_proj"):
                    act.wait_ge(misc_full, m + 1)
                    high_part(arg, 0 if kind == "q_proj" else 1, src)
                elif kind == "on_turn":
                    act.wait_ge(misc_full, m + 1)
                    if arg >= 1:
                        act.wait_ge(misc_full, number["wo", arg - 1] + 1)
                    nc.scalar.activation(onT[:], src, ACT.Copy).then_inc(on_turned, 1)
                    act.wait_ge(on_turned, arg + 1)
                    act.sem_inc(misc_empty, 1)
                elif kind == "wo":
                    act.wait_ge(misc_full, m + 1)
                    nc.scalar.activation(s_all[:, QT * arg:QT * (arg + 1), :],
                                         src.rearrange("p (c d) -> p c d", d=D), ACT.Copy).then_inc(s_ready, 1)
                    act.wait_ge(s_ready, arg + 1)
                    act.sem_inc(misc_empty, 1)

            def relu_half(j, par):
                act.wait_ge(h_full, j + 1)
                for c in range(FC // 2):
                    cc = c + FC // 2
                    last = nc.scalar.activation(hid[par][:, P * cc:P * (cc + 1)], ps[:, 2 * par + 1, P * c:P * (c + 1)],
                                                ACT.Relu, bias=stage1[par][:, F + cc:F + cc + 1])
                last.then_inc(h_act, 1)

            act.wait_ge(qk0_full, 1)
            high_part(0, 0, bank(4))
            act.wait_ge(qk0_full, 2)
            high_part(0, 1, bank(5))
            for b in range(B):
                values(b)
            for t in range(END + 1):
                if t == FFN_AT:
                    for n in range(1, TURNS, 2):
                        act.wait_ge(z_turned, n + 1)
                        w = P * (min(4 * n + 4, NS) - 4 * n)
                        nc.scalar.activation(zT[:, 4 * P * n:4 * P * n + w], ps[:, n, 0:w], ACT.Copy
                                             ).then_inc(zT_act, 1)
                    relu_half(0, 0)
                    with act.Fori(0, (NS - 1) // 2) as i:
                        relu_half(2 * i + 1, 1)
                        relu_half(2 * i + 2, 0)
                if t < STEPS:
                    exponentials(t, 0)
                    exponentials(t, 1)
                if t >= 1:
                    for kind, arg in tasks_at(t - 1):
                        task(kind, arg)
                if t == 2:
                    act.wait_ge(amax_done, 1)
                    nc.scalar.activation(ea[:], amax[:], ACT.Exp, scale=-1.0).then_inc(ea_done, 1)
                if t < STEPS:
                    exponentials(t, 2)
                    exponentials(t, 3)
                for b in range(B):
                    if t == gate_at(b):
                        act.wait_ge(gate_in, b + 1)
                        nc.scalar.activation(gtmp[:, b % 2, :].rearrange("p (c d) -> p c d", d=D),
                                             zrow[:, QT * b:QT * (b + 1), 0:D], ACT.Exp, scale=-1.0
                                             ).then_inc(gate_exp, 1)

        @block.gpsimd
        def _(pool):
            steps = [0]

            def link(ins):
                steps[0] += 1
                ins.then_inc(pool_step, 1)
                pool.wait_ge(pool_step, steps[0])

            def rsqrt(b, m, v, r, done):
                c = slice(QT * b, QT * (b + 1))
                link(nc.gpsimd.tensor_scalar(v[:, c], m[:, c, 1], EPS, None, ALU.add))
                nc.gpsimd.tensor_tensor(r[:, c], v[:, c], mhalf[:, c], ALU.pow).then_inc(done, 1)

            def mask(t):
                u, kt = divmod(t, QT)
                lo, hi = q_tiles(kt)
                pool.wait_ge(exp_done, 4 * t + 4)
                w = P * (hi - lo)
                last = None
                if kt > 0:
                    v = probs[:, t % RING, :, 0:P]
                    last = nc.gpsimd.affine_select(out=v, in_=v, compare_op=ALU.is_ge, fill=0.0, base=0,
                                                   pattern=[[0, 4], [1, P]], channel_multiplier=-1)
                    if kt == QT - 1:
                        last.then_inc(p_masked, 1)
                if kt < QT - 1:
                    v = probs[:, t % RING, :, w - P:w]
                    nc.gpsimd.affine_select(out=v, in_=v, compare_op=ALU.is_ge, fill=0.0, base=0,
                                            pattern=[[0, 4], [-1, P]], channel_multiplier=1).then_inc(p_masked, 1)

            def stage_1(j, par):
                e = pool.value_load(expert[0:1, bass.ds(j, 1)], min_val=0, max_val=E - 1)
                nc.gpsimd.tensor_copy(stage1[par], wall_flat[:, bass.ds(e * WW, ST1)]).then_inc(w1_staged, 1)

            def stage_2(j, par):
                e = pool.value_load(expert[0:1, bass.ds(j, 1)], min_val=0, max_val=E - 1)
                nc.gpsimd.tensor_copy(stage2[par], wall_flat[:, bass.ds(e * WW + O_W2, ST2)]).then_inc(w2_staged, 1)

            def send_y(j, par):
                if not isinstance(j, int):
                    pool.wait_ge(y_sent[par], 8 * (j - par))
                elif j >= 2:
                    pool.wait_ge(y_sent[par], 16 * (j // 2))
                nc.gpsimd.tensor_copy(dest1[:, par, :], dest[:, bass.ds(j, 1)]).then_inc(dest_staged, 1)
                pool.wait_ge(dest_staged, j + 1)
                pool.wait_ge(y_copied, j + 1)
                pool.sem_inc(sending, 1)
                nc.gpsimd.indirect_dma_start(
                    out=f_dram, out_offset=bass.IndirectOffsetOnAxis(ap=dest1[:, par, :].bitcast(U32), axis=0),
                    in_=ysb[:, par, :], in_offset=None).then_inc(y_sent[par], 16)

            def tile_work(j, par):
                pool.wait_ge(h_dve, j + 1)
                pool.wait_ge(h_act, j + 1)
                stage_1(j + 2, par)
                send_y(j, par)
                stage_2(j + 2, par)

            def feed_forward():
                pool.wait_ge(z_turned, TURNS)
                pool.wait_ge(experts_done, 1)
                for j in range(2):
                    stage_1(j, j)
                    stage_2(j, j)
                tile_work(0, 0)
                tile_work(1, 1)
                with pool.Fori(1, NS // 2) as i:
                    tile_work(2 * i, 0)
                    tile_work(2 * i + 1, 1)
                send_y(NS - 1, (NS - 1) % 2)

            nc.gpsimd.memset(mhalf[:], -0.5).then_inc(pool_step, 1)
            steps[0] += 1
            pool.wait_ge(pool_step, steps[0])
            nc.gpsimd.memset(raw(qst), 0.0).then_inc(qst_zero, 1)
            for b in range(B):
                pool.wait_ge(var_done, b + 1)
                rsqrt(b, mv, vare, rstd, rstd_done)
            pool.wait_ge(rstd_done, B)
            nc.gpsimd.memset(raw(kst[96:128, :, :, :]), 1.0).then_inc(kst_ones, 1)
            pool.wait_ge(kst_ones, 1)
            link(nc.gpsimd.memset(before[:], 1.0))
            nc.gpsimd.affine_select(out=before[:], in_=before[:], compare_op=ALU.is_gt, fill=0.0, base=0,
                                    pattern=[[1, P]], channel_multiplier=-1).then_inc(consts_set, 1)
            nc.gpsimd.iota(firstw[:], [[-1, E]], base=E, channel_multiplier=0,
                           allow_small_or_imprecise_dtypes=True).then_inc(consts_set, 1)
            pool.wait_ge(consts_set, 4)
            nc.gpsimd.iota(starts[:], [[P, NS + 1], [0, E]], base=0, channel_multiplier=0,
                           allow_small_or_imprecise_dtypes=True).then_inc(consts_set, 1)
            pool.wait_ge(consts_set, 5)
            nc.gpsimd.iota(zrow[:, :, D:ROW].bitcast(I32), [[P, NT], [0, 1]], base=0, channel_multiplier=1
                           ).then_inc(consts_set, 1)
            nc.gpsimd.memset(zs[:, :, 0:D], 0.0).then_inc(pre_made, 1)
            nc.gpsimd.iota(zs[:, :, D:ROW].bitcast(I32), [[P, NS], [0, 1]], base=T, channel_multiplier=1
                           ).then_inc(pre_made, 1)
            for t in range(END + 1):
                if t < STEPS:
                    if t == FFN_AT:
                        feed_forward()
                    mask(t)
                if 3 <= t < 3 + B:
                    b = t - 3
                    pool.wait_ge(var2_done, b + 1)
                    rsqrt(b, mv2, vare2, rstd2, rstd2_done)
                    pool.wait_ge(rstd2_done, b + 1)
                    for c in range(QT * b, QT * (b + 1)):
                        last = nc.gpsimd.tensor_scalar(zrow[:, c, 0:D], xn[:, c, :], mv2[:, c, 0:1],
                                                       rstd2[:, c:c + 1], ALU.subtract, ALU.mult)
                    last.then_inc(z_done, 1)
                if 7 <= t < 15:
                    if t == 7:
                        pool.wait_ge(slots_done, 1)
                        pool.wait_ge(z_done, B)
                        pool.wait_ge(z_cleared, 16)
                        pool.wait_ge(consts_set, 6)
                    for c in range(2 * (t - 7), 2 * (t - 7) + 2):
                        nc.gpsimd.indirect_dma_start(
                            out=z_dram, out_offset=bass.IndirectOffsetOnAxis(ap=slot[:, c:c + 1].bitcast(U32), axis=0),
                            in_=zrow[:, c, :], in_offset=None).then_inc(z_sent, 16)
                if 15 <= t < 19:
                    if t == 15:
                        pool.wait_ge(b1_done, 1)
                    for e in range(2 * (t - 15), 2 * (t - 15) + 2):
                        w = wall[:, e, 0:F]
                        nc.gpsimd.tensor_scalar(w, w, lng[:, e:e + 1], None, ALU.mult).then_inc(w1_folded, 1)
                if t == FFN_AT - 3:
                    pool.wait_ge(zs_in, 16)
                    nc.gpsimd.tensor_copy(dest[:].unsqueeze(2), zs[:, :, D:ROW].bitcast(I32)).then_inc(dest_copied, 1)
                    pool.wait_ge(dest_copied, 1)
                    pool.wait_ge(w1_folded, E)
                for b in range(B):
                    zb = zrow[:, QT * b:QT * (b + 1), 0:D]
                    gt = gtmp[:, b % 2, :].rearrange("p (c d) -> p c d", d=D)
                    if t == gate_at(b) - 1:
                        pool.wait_ge(f_in[b], 16)
                        pool.wait_ge(alpha_done, 1)
                        al = alpha[:, QT * b:QT * (b + 1)].unsqueeze(2).broadcast_to([P, QT, D])
                        link(nc.gpsimd.tensor_tensor(zb, zb, al, ALU.mult))
                        nc.gpsimd.tensor_tensor(zb, zb, xn[:, QT * b:QT * (b + 1), :], ALU.add).then_inc(gate_in, 1)
                    if t == gate_at(b):
                        pool.wait_ge(gate_exp, b + 1)
                        nc.gpsimd.tensor_scalar(gtmp[:, b % 2, :], gtmp[:, b % 2, :], 1.0, None, ALU.add
                                                ).then_inc(gate_plus, 1)
                    if t == gate_at(b) + 2:
                        pool.wait_ge(gate_rec, b + 1)
                        nc.gpsimd.tensor_tensor(zb, zb, gt, ALU.mult).then_inc(gate_done, 1)
                        pool.wait_ge(gate_done, b + 1)
                        pool.dma_start(xn[:, QT * b:QT * (b + 1), :], x_tok[:, QT * b:QT * (b + 1), :]
                                       ).then_inc(x_again[b], 16)
                    wo_at = [tt for tt, k, a in tasks if (k, a) == ("wo", b)][0]
                    if t == max(wo_at + 2, gate_at(b) + 4) or (t == END and wo_at + 2 > END):
                        pool.wait_ge(s_ready, b + 1)
                        pool.wait_ge(x_again[b], 16)
                        sv = s_all[:, QT * b:QT * (b + 1), :]
                        link(nc.gpsimd.tensor_tensor(sv, sv, zb, ALU.mult))
                        nc.gpsimd.tensor_tensor(sv, sv, xn[:, QT * b:QT * (b + 1), :], ALU.add).then_inc(res_done, 1)


_INS = ["x", "wq_t", "wk_t", "wv_t", "wo_t", "cent_t", "ln_g_t", "ln_b_t", "w1_t", "b1_t", "w2_t", "b2", "ident_in"]


def kernel(**inputs):
    import numpy as np
    import concourse.bacc as bacc
    from concourse.bass_utils import run_bass_kernel_spmd as run

    a = {k.split("_", 1)[1]: np.asarray(v) for k, v in inputs.items()}
    x = a["attn_x"]
    E, F, D = a["ffn_w1"].shape
    laid = {
        "x": x.reshape(-1, D),
        "wq_t": a["attn_Wq"].T, "wk_t": a["attn_Wk"].T, "wv_t": a["attn_Wv"].T, "wo_t": a["attn_Wo"].T,
        "cent_t": a["ffn_centroids"].T, "ln_g_t": a["ffn_ln_g"].T, "ln_b_t": a["ffn_ln_b"].T,
        "w1_t": a["ffn_w1"].transpose(2, 0, 1),
        "b1_t": a["ffn_b1"].reshape(E, F // 128, 128).transpose(2, 0, 1),
        "w2_t": a["ffn_w2"].transpose(2, 0, 1).reshape(F // 128, 128, E, D).transpose(1, 2, 0, 3).reshape(128, E, -1),
        "b2": a["ffn_b2"],
        "ident_in": np.eye(128, dtype=np.float32),
    }
    nc = bacc.Bacc("TRN2", target_bir_lowering=False, num_devices=1)
    arrays, args = {}, []
    for name in _INS:
        v = np.ascontiguousarray(laid[name])
        arrays[f"in_{name}_dram"] = v
        args.append(nc.dram_tensor(f"in_{name}_dram", v.shape, mybir.dt.from_np(v.dtype), kind="ExternalInput").ap())
    args.append(nc.dram_tensor("out_0_dram", (x.shape[0] * x.shape[1], D), F32, kind="ExternalOutput").ap())
    build(nc, *args)
    r = run(nc, [arrays], core_ids=[0])
    return r.results[0]["out_0_dram"].reshape(x.shape)
```

```python
from contextlib import ExitStack

import concourse.bass as bass
from concourse import mybir

ALU = mybir.AluOpType
ACT = mybir.ActivationFunctionType
AX = mybir.AxisListType
F32 = mybir.dt.float32
F32R = mybir.dt.float32r
BF16 = mybir.dt.bfloat16
I32 = mybir.dt.int32
U32 = mybir.dt.uint32

P = 128


def build(nc, x, w_attn, small, w_ffn, b2, ident_in, out):
    T, D = x.shape
    B = 4
    S = T // B
    NT = T // P
    QT = S // P
    DH = 8
    H = D // DH
    G = H // 4
    SCALE = DH ** -0.5
    E = b2.shape[0]
    F = 512
    FC = F // P
    EPS = 1e-5
    NS = (T - E) // P + E
    NX = NS + 2
    ROW = D + 1
    UNITS = B * G
    STEPS = UNITS * QT
    LAG = 2
    QRING = 6
    RING = 3
    VW = DH + 1
    BASE0 = QT * 2
    FFN_AT = STEPS // 2
    W1W, B1W, W2W = F, FC, FC * D
    O_B1, O_W2, O_B2 = W1W, W1W + B1W, W1W + B1W + W2W
    WW = O_B2 + D
    ST1 = W1W + B1W
    ST2 = W2W + D

    def q_tiles(kt):
        return max(0, kt - 1), min(QT, kt + 2)

    tasks = []
    for t in range(-1, STEPS + 8):
        u, kt = divmod(t, QT)
        g, b = u % G, u // G
        if t == -1:
            tasks += [(t, "max_t", 0), (t, "max_t", 1)]
            continue
        if t == 0:
            tasks.append((t, "affinity", 0))
        if t == 2:
            tasks.append((t, "prefix", 0))
        if t == 5:
            tasks.append((t, "bias1", 0))
        if kt == 0 and 1 <= u and u + 1 < UNITS:
            tasks.append((t, "max_t", u + 1))
        if kt == 1 and g == 0 and b + 1 < B:
            tasks.append((t, "q_proj", b + 1))
        if kt == 3 and g == 0 and b + 1 < B:
            tasks.append((t, "k_proj", b + 1))
        if kt == 2 and 1 <= u <= UNITS:
            tasks.append((t, "o_turn", u - 1))
        if kt == 1 and g == 1 and b >= 1:
            tasks.append((t, "on_turn", b - 1))
        if kt == 3 and g == 1 and b >= 1:
            tasks.append((t, "wo", b - 1))
    TURNS = (NS + 3) // 4
    assert TURNS == 6 and len({t for t, _, _ in tasks if t >= 0}) == len(tasks) - 2
    number = {(kind, arg): m for m, (_, kind, arg) in enumerate(tasks)}
    END = max(t for t, _, _ in tasks) + 1

    def tasks_at(t):
        return [(kind, arg) for at, kind, arg in tasks if at == t]

    with ExitStack() as ctx:
        def sb(name, shape, dt=F32):
            return ctx.enter_context(nc.sbuf_tensor(name, shape, dt)).ap()

        def sem(name):
            return ctx.enter_context(nc.semaphore(name))

        ident = sb("ident", [P, P])
        before = sb("before", [P, P], BF16)
        ones_b = sb("ones_b", [P, P], BF16)
        xn = sb("xn", [P, NT, D])
        zrow = sb("zrow", [P, NT, ROW])
        xnT = sb("xnT", [P, T])
        wqk = sb("wqk", [P, 4, D])
        features = sb("features", [P, 3, E])
        cent, lng, lnb = (features[:, n, :] for n in range(3))
        wall = sb("wall", [P, E, WW])
        wall_flat = wall.rearrange("p e w -> p (e w)")
        vp = sb("vp", [P, NT * H * VW + 32 - VW])
        qhl = sb("qhl", [P, 2, S], F32R)
        khl = sb("khl", [P, 2, S], F32R)
        qst = sb("qst", [P, QRING, 4, S], F32R)
        kst = sb("kst", [P, 2, G, S], F32R)
        mneg = sb("mneg", [P, 2, 4 * QT])
        mT = sb("mT", [4 * QT, 2, P], F32R)
        probs = sb("probs", [P, RING, 4, 3 * P])
        oT = sb("oT", [P, 2, S])
        rden = sb("rden", [P, 2, QT, 4])
        on = sb("on", [P, QT, D])
        onT = sb("onT", [P, S])
        s0 = sb("s0", [P, QT, D])
        gtmp = sb("gtmp", [P, 2, QT * D])
        stats = sb("stats", [P, NT, 6])
        mv = sb("mv", [P, NT, 2])
        vare = sb("vare", [P, NT])
        rstd = sb("rstd", [P, NT])
        mv2 = sb("mv2", [P, NT, 2])
        rstd2 = sb("rstd2", [P, NT])
        mhalf = sb("mhalf", [P, NT])
        pool_ws = sb("pool_ws", [P, 2 * ST1 + 2 * ST2 + 2 * F])
        zs = pool_ws[:, 0:NS * ROW].rearrange("p (j r) -> p j r", r=ROW)
        o = 0
        stage1, stage2, hid = [], [], []
        for par in range(2):
            stage1.append(pool_ws[:, o:o + ST1])
            o += ST1
        for par in range(2):
            stage2.append(pool_ws[:, o:o + ST2])
            o += ST2
        for par in range(2):
            hid.append(pool_ws[:, o:o + F])
            o += F
        zT = sb("zT", [P, NS * P])
        s_of = [s0] + [zT[:, S * (b - 1):S * b].rearrange("p (c d) -> p c d", d=D) for b in range(1, B)]
        dest = sb("dest", [P, NS], I32)
        dest1 = sb("dest1", [P, 2, 1], I32)
        ysb = sb("ysb", [P, 2, D])
        aff = sb("aff", [P, NT, E])
        amax = sb("amax", [P, NT])
        alpha = sb("alpha", [P, NT])
        ea = sb("ea", [P, NT])
        firstw = sb("firstw", [P, E])
        oneh = sb("oneh", [P, E, NT])
        rowtot = sb("rowtot", [P, E], BF16)
        oneF = sb("oneF", [P, E * NT])
        scan = sb("scan", [P, E, NT])
        pre = sb("pre", [P, 2 * E])
        npad_f = sb("npad_f", [P, E])
        npad_i = sb("npad_i", [P, E], I32)
        npad_j = sb("npad_j", [P, E], I32)
        npad = sb("npad", [P, E])
        ends = sb("ends", [P, E])
        offs = sb("offs", [P, E])
        slotf = sb("slotf", [P, NT])
        slot = sb("slot", [P, NT], I32)
        starts = sb("starts", [1, NX, E])
        expf = sb("expf", [1, NX])
        expert = sb("expert", [1, NX], I32)
        ps = ctx.enter_context(nc.psum_tensor("ps", [P, 8, 512], F32))
        ST, SM, PV, MISC = 0, 2, 6, 7

        z_dram = nc.dram_tensor("z_dram", (NS * P, ROW), F32, kind="Internal").ap()
        f_dram = nc.dram_tensor("f_dram", (T + NS * P, D), F32, kind="Internal").ap()

        x_in = [sem(f"x_in{b}") for b in range(B)]
        ident_in_s = sem("ident_in_s")
        proj_in = sem("proj_in")
        small_in = sem("small_in")
        w_in = sem("w_in")
        consts_set = sem("consts_set")
        vp_set = sem("vp_set")
        qst_zero = sem("qst_zero")
        kst_ones = sem("kst_ones")
        var_done = sem("var_done")
        rstd_done = sem("rstd_done")
        xn_done = sem("xn_done")
        stat_step = sem("stat_step")
        xnT_full = sem("xnT_full")
        xnT_done = sem("xnT_done")
        v_full = sem("v_full")
        v_done = sem("v_done")
        qk0_full = sem("qk0_full")
        hi_done = sem("hi_done")
        lo_done = sem("lo_done")
        q_placed = [sem(f"q_placed{r}") for r in range(QRING // 2)]
        k_placed = [sem(f"k_placed{r}") for r in range(2)]
        s_full = sem("s_full")
        s_max = sem("s_max")
        m_turned = sem("m_turned")
        m_placed = [sem(f"m_placed{r}") for r in range(QRING)]
        st_full = sem("st_full")
        exp_done = sem("exp_done")
        p_masked = sem("p_masked")
        pv_done = sem("pv_done")
        pv_copied = sem("pv_copied")
        misc_full = sem("misc_full")
        misc_empty = sem("misc_empty")
        rden_done = sem("rden_done")
        o_normed = sem("o_normed")
        on_turned = sem("on_turned")
        s_ready = sem("s_ready")
        aff_done = sem("aff_done")
        amax_done = sem("amax_done")
        ea_done = sem("ea_done")
        alpha_done = sem("alpha_done")
        route = sem("route")
        rowtot_done = sem("rowtot_done")
        slots_done = sem("slots_done")
        experts_done = sem("experts_done")
        pre_made = sem("pre_made")
        z_cleared = sem("z_cleared")
        var2_done = sem("var2_done")
        rstd2_done = sem("rstd2_done")
        z_done = sem("z_done")
        z_sent = sem("z_sent")
        zs_in = sem("zs_in")
        dest_copied = sem("dest_copied")
        z_turned = sem("z_turned")
        zT_dve = sem("zT_dve")
        zT_act = sem("zT_act")
        b1_done = sem("b1_done")
        w1_folded = sem("w1_folded")
        w1_staged = sem("w1_staged")
        w2_staged = sem("w2_staged")
        dest_staged = sem("dest_staged")
        sending = sem("sending")
        h_full = sem("h_full")
        h_dve = sem("h_dve")
        h_act = sem("h_act")
        y_full = sem("y_full")
        y_copied = sem("y_copied")
        y_sent = [sem(f"y_sent{r}") for r in range(2)]
        f_in = [sem(f"f_in{b}") for b in range(B)]
        x_again = [sem(f"x_again{b}") for b in range(B)]
        gate_in = sem("gate_in")
        gate_exp = sem("gate_exp")
        gate_plus = sem("gate_plus")
        gate_rec = sem("gate_rec")
        gate_done = sem("gate_done")
        pool_step = sem("pool_step")
        res_done = sem("res_done")
        stored = sem("stored")

        def bank(n):
            return ps[:, n, :]

        def gate_at(b):
            return FFN_AT + 3 + 4 * b

        def raw(ap):
            return ap.bitcast(F32)

        def lhs_v(tile, h):
            o = (tile * H + h) * VW
            return vp[:, o:o + 32]

        def s_width(qt):
            lo, hi = q_tiles(qt)
            return (hi - lo) * P

        x_tok = x.rearrange("(c p) d -> p c d", p=P)
        out_tok = out.rearrange("(c p) d -> p c d", p=P)
        f_tok = f_dram[0:T, :].rearrange("(c p) d -> p c d", p=P)

        block = ctx.enter_context(nc.Block())

        @block.sync
        def _(sp):
            def load_x(b):
                sp.dma_start(xn[:, QT * b:QT * (b + 1), :], x_tok[:, QT * b:QT * (b + 1), :]).then_inc(x_in[b], 16)

            load_x(0)
            sp.dma_start(ident[:], ident_in).then_inc(ident_in_s, 16)
            sp.dma_start(wqk, w_attn).then_inc(proj_in, 16)
            for b in range(1, B):
                load_x(b)
            sp.dma_start(features, small).then_inc(small_in, 16)

            def place_q(pair):
                b, half, r = pair // 2, pair % 2, 2 * pair % QRING
                sp.wait_ge(lo_done, 2 * b + 1)
                if pair < QRING // 2:
                    sp.wait_ge(qst_zero, pair + 1)
                else:
                    sp.wait_ge(st_full, 16 * (2 * pair - QRING + 2))
                for slot_n, part in enumerate((0, 0, 1)):
                    for j in range(4):
                        sp.dma_start(raw(qst[32 * slot_n + 8 * j:32 * slot_n + 8 * j + 8, r:r + 2, j, :]),
                                     raw(qhl[64 * half + 16 * j:64 * half + 16 * j + 16, part, :])
                                     ).then_inc(q_placed[pair % (QRING // 2)], 16)

            def place_k(b):
                sp.wait_ge(lo_done, 2 * b + 2)
                if b >= 2:
                    sp.wait_ge(st_full, 16 * G * (b - 1))
                for slot_n, part in enumerate((0, 1, 0)):
                    sp.dma_start(raw(kst[32 * slot_n:32 * slot_n + 32, b % 2, :, :]),
                                 raw(khl[:, part, :])).then_inc(k_placed[b % 2], 16)

            def place_m(u):
                sp.wait_ge(m_turned, u + 1)
                if u >= QRING:
                    sp.wait_ge(st_full, 16 * (u - QRING + 1))
                sp.dma_start(raw(qst[96:97, u % QRING, :, :]), raw(mT[:, u % 2, :])).then_inc(m_placed[u % QRING], 16)

            place_q(0)
            place_k(0)
            place_q(1)
            sp.dma_start(wall[:, :, 0:O_B2], w_ffn).then_inc(w_in, 16)
            sp.dma_start(wall[:, :, O_B2:WW], b2.partition_broadcast(P)).then_inc(w_in, 16)
            place_m(0)
            place_m(1)
            sp.wait_ge(pre_made, 2)
            sp.dma_start(z_dram.rearrange("(j p) r -> p j r", p=P), zs).then_inc(z_cleared, 16)
            for u in range(UNITS):
                if u % 2 == 0 and u + 4 < UNITS:
                    place_q(u // 2 + 2)
                if u % G == 0 and u + G < UNITS:
                    place_k(u // G + 1)
                if u + 2 < UNITS:
                    place_m(u + 2)
                if u == 4:
                    sp.wait_ge(z_sent, 16 * NT)
                    sp.dma_start(zs, z_dram.rearrange("(j p) r -> p j r", p=P)).then_inc(zs_in, 16)
                if u == FFN_AT // QT - 1:
                    sp.wait_ge(y_sent[0], 16 * ((NS + 1) // 2))
                    sp.wait_ge(y_sent[1], 16 * (NS // 2))
                    for c in range(B):
                        sp.dma_start(zrow[:, QT * c:QT * (c + 1), 0:D], f_tok[:, QT * c:QT * (c + 1), :]
                                     ).then_inc(f_in[c], 16)
            for b in range(B):
                sp.wait_ge(res_done, b + 1)
                sp.dma_start(out_tok[:, QT * b:QT * (b + 1), :], s_of[b]).then_inc(stored, 16)
            sp.wait_ge(stored, 16 * B)

        @block.tensor
        def _(pe):
            def turn_x(b):
                pe.wait_ge(xn_done, b + 1)
                for c in range(QT):
                    mm = nc.tensor.transpose(ps[:, b, P * c:P * (c + 1)], xn[:, QT * b + c, :], ident[:])
                mm.then_inc(xnT_full, 1)

            def project(dst, w, b):
                return nc.tensor.matmul(dst, wqk[:, w, :], xnT[:, S * b:S * (b + 1)], start=True, stop=True)

            def values(b):
                pe.wait_ge(xnT_done, b + 1)
                if b >= 2:
                    pe.wait_ge(v_done, b - 1)
                for c in range(QT):
                    mm = nc.tensor.matmul(ps[:, 6 + b % 2, P * c:P * (c + 1)],
                                          xnT[:, S * b + P * c:S * b + P * (c + 1)], wqk[:, 2, :],
                                          start=True, stop=True)
                mm.then_inc(v_full, 1)

            def maxima_item(n):
                u, rest = divmod(n, 2 * QT)
                qt, jj = divmod(rest, 2)
                b, g, r = u // G, u % G, u % QRING
                lo, hi = q_tiles(qt)
                if rest == 0:
                    pair, nr = u // 2, QRING // 2
                    pe.wait_ge(q_placed[pair % nr], 16 * 12 * (pair // nr + 1))
                    pe.wait_ge(k_placed[b % 2], 16 * 3 * (b // 2 + 1))
                if n >= 2:
                    pe.wait_ge(s_max, n - 1)
                for i in range(2):
                    mm = nc.tensor.matmul(ps[:, SM + 2 * (n % 2) + i, 0:P * (hi - lo)],
                                          qst[0:96, r, 2 * jj + i, P * qt:P * (qt + 1)],
                                          kst[0:96, b % 2, g, P * lo:P * hi], start=True, stop=True)
                mm.then_inc(s_full, 1)

            def score(t, j):
                u, kt = divmod(t, QT)
                b, g = u // G, u % G
                n = 4 * t + j
                lo, hi = q_tiles(kt)
                if kt == 0 and j == 0:
                    pe.wait_ge(m_placed[u % QRING], 16 * (u // QRING + 1))
                    if u == 0:
                        pe.wait_ge(kst_ones, 1)
                if n >= 2:
                    pe.wait_ge(exp_done, n - 1)
                nc.tensor.matmul(ps[:, ST + n % 2, 0:P * (hi - lo)], kst[0:97, b % 2, g, P * kt:P * (kt + 1)],
                                 qst[0:97, u % QRING, j, P * lo:P * hi], start=True, stop=True).then_inc(st_full, 1)

            def weighted(t):
                u, kt = divmod(t, QT)
                b, g = u // G, u % G
                lo, hi = q_tiles(kt)
                pe.wait_ge(p_masked, t + 1)
                if kt == 0 and u >= 1:
                    pe.wait_ge(pv_copied, u)
                for j in range(4):
                    mm = nc.tensor.matmul(ps[32 * j:32 * j + 32, PV, P * lo:P * hi],
                                          lhs_v(QT * b + kt, 4 * g + j), probs[:, t % RING, j, 0:P * (hi - lo)],
                                          start=(kt == 0), stop=(kt == QT - 1), skip_group_check=True)
                mm.then_inc(pv_done, 1)

            def task(kind, arg):
                m = number[kind, arg]
                if m >= 1:
                    pe.wait_ge(misc_empty, m)
                dst = bank(MISC)
                if kind == "max_t":
                    pe.wait_ge(s_max, 2 * QT * (arg + 1))
                    mm = nc.tensor.transpose(dst[0:4 * QT, 0:P], mneg[:, arg % 2, :], ident[:])
                elif kind == "affinity":
                    pe.wait_ge(small_in, 16)
                    for c in range(NT):
                        mm = nc.tensor.matmul(dst[:, E * c:E * (c + 1)], xnT[:, P * c:P * (c + 1)], cent[:],
                                              start=True, stop=True)
                elif kind == "prefix":
                    pe.wait_ge(rowtot_done, 1)
                    pe.wait_ge(consts_set, 6)
                    nc.tensor.matmul(dst[:, 0:E], before[:], rowtot[:], start=True, stop=True)
                    mm = nc.tensor.matmul(dst[:, E:2 * E], ones_b[:], rowtot[:], start=True, stop=True)
                elif kind == "bias1":
                    pe.wait_ge(w_in, 32)
                    for e in range(E):
                        for c in range(FC):
                            mm = nc.tensor.matmul(dst[:, FC * e + c:FC * e + c + 1],
                                                  wall[:, e, P * c:P * (c + 1)], lnb[:, e:e + 1],
                                                  start=True, stop=True)
                elif kind == "q_proj":
                    mm = project(dst, 0, arg)
                elif kind == "k_proj":
                    mm = project(dst, 1, arg)
                elif kind == "o_turn":
                    pe.wait_ge(pv_copied, arg + 1)
                    for qt in range(QT):
                        mm = nc.tensor.transpose(dst[:, P * qt:P * (qt + 1)], oT[:, arg % 2, P * qt:P * (qt + 1)],
                                                 ident[:])
                elif kind == "on_turn":
                    pe.wait_ge(o_normed, G * (arg + 1))
                    for qt in range(QT):
                        mm = nc.tensor.transpose(dst[:, P * qt:P * (qt + 1)], on[:, qt, :], ident[:])
                elif kind == "wo":
                    pe.wait_ge(on_turned, arg + 1)
                    for qt in range(QT):
                        mm = nc.tensor.matmul(dst[:, P * qt:P * (qt + 1)], onT[:, P * qt:P * (qt + 1)], wqk[:, 3, :],
                                              start=True, stop=True)
                mm.then_inc(misc_full, 1)

            def hidden(j, par):
                pe.wait_ge(w1_staged, j + 1)
                if not isinstance(j, int) or j >= 2:
                    pe.wait_ge(h_dve, j - 1)
                    pe.wait_ge(h_act, j - 1)
                for c in range(FC):
                    mm = nc.tensor.matmul(ps[:, 2 * par + c // 2, P * (c % 2):P * (c % 2) + P],
                                          stage1[par][:, P * c:P * (c + 1)], zT[:, bass.ds(j * P, P)],
                                          start=True, stop=True)
                mm.then_inc(h_full, 1)

            def output(j, par):
                pe.wait_ge(w2_staged, j + 1)
                pe.wait_ge(h_dve, j + 1)
                pe.wait_ge(h_act, j + 1)
                if not isinstance(j, int) or j >= 2:
                    pe.wait_ge(y_copied, j - 1)
                for c in range(FC):
                    mm = nc.tensor.matmul(ps[:, 4 + par, 0:P], hid[par][:, P * c:P * (c + 1)],
                                          stage2[par][:, P * c:P * (c + 1)], start=(c == 0), stop=(c == FC - 1))
                mm.then_inc(y_full, 1)

            def feed_forward():
                pe.wait_ge(exp_done, 4 * FFN_AT)
                pe.wait_ge(s_max, BASE0 * (FFN_AT // QT + 2))
                pe.wait_ge(zs_in, 16)
                for n in range(TURNS):
                    for c in range(4 * n, min(4 * n + 4, NS)):
                        mm = nc.tensor.transpose(ps[:, n, P * (c % 4):P * (c % 4) + P], zs[:, c, 0:D], ident[:])
                    mm.then_inc(z_turned, 1)
                pe.wait_ge(zT_dve, TURNS // 2)
                pe.wait_ge(zT_act, TURNS // 2)
                hidden(0, 0)
                hidden(1, 1)
                output(0, 0)
                hidden(2, 0)
                output(1, 1)
                with pe.Fori(1, NS // 2) as i:
                    hidden(2 * i + 1, 1)
                    output(2 * i, 0)
                    hidden(2 * i + 2, 0)
                    output(2 * i + 1, 1)
                output(NS - 1, (NS - 1) % 2)
                pe.wait_ge(y_copied, NS)

            pe.wait_ge(ident_in_s, 16)
            turn_x(0)
            pe.wait_ge(xnT_done, 1)
            pe.wait_ge(proj_in, 16)
            project(bank(4), 0, 0).then_inc(qk0_full, 1)
            project(bank(5), 1, 0).then_inc(qk0_full, 1)
            values(0)
            for b in range(1, B):
                turn_x(b)
                values(b)
            pe.wait_ge(xnT_done, B)
            pe.wait_ge(lo_done, 2)
            pe.wait_ge(v_done, B)
            for n in range(2 * BASE0):
                maxima_item(n)
            for kind, arg in tasks_at(-1):
                task(kind, arg)
            for t in range(END):
                if t == FFN_AT:
                    feed_forward()
                more = t < STEPS - 2 * QT
                if t < STEPS:
                    score(t, 0)
                    score(t, 1)
                    if more:
                        maxima_item(2 * BASE0 + 2 * t)
                    score(t, 2)
                    if more:
                        maxima_item(2 * BASE0 + 2 * t + 1)
                    score(t, 3)
                if LAG <= t < STEPS + LAG:
                    weighted(t - LAG)
                for kind, arg in tasks_at(t):
                    task(kind, arg)

        @block.vector
        def _(dve):
            steps = [0]

            def link(ins):
                steps[0] += 1
                ins.then_inc(route, 1)
                dve.wait_ge(route, steps[0])

            def moments(b, src, st, m):
                for c in range(QT * b, QT * (b + 1)):
                    nc.vector.bn_stats(st[:, c, :], src[:, c, 0:D]).then_inc(stat_step, 1)
                dve.wait_ge(stat_step, stat_count(QT))
                for c in range(QT * b, QT * (b + 1)):
                    last = nc.vector.bn_aggr(m[:, c, :], st[:, c, :])
                return last

            counted = [0]

            def stat_count(n):
                counted[0] += n
                return counted[0]

            def norm(b):
                dve.wait_ge(rstd_done, b + 1)
                for c in range(QT * b, QT * (b + 1)):
                    last = nc.vector.tensor_scalar(xn[:, c, :], xn[:, c, :], mv[:, c, 0:1], rstd[:, c:c + 1],
                                                   ALU.subtract, ALU.mult)
                last.then_inc(xn_done, 1)

            def copy_xT(b):
                dve.wait_ge(xnT_full, b + 1)
                nc.vector.tensor_copy(xnT[:, S * b:S * (b + 1)], bank(b)).then_inc(xnT_done, 1)

            def low_part(b, which, src):
                dve.wait_ge(hi_done, 2 * b + which + 1)
                hl = (qhl, khl)[which]
                return nc.vector.tensor_tensor(hl[:, 1, :], src, hl[:, 0, :].bitcast(F32), ALU.subtract)

            def maxima(n):
                u, rest = divmod(n, 2 * QT)
                qt, jj = divmod(rest, 2)
                dve.wait_ge(s_full, n + 1)
                if rest == 0 and u >= 2:
                    dve.wait_ge(misc_full, number["max_t", u - 2] + 1)
                dst = mneg[:, u % 2, :].rearrange("p (j q) -> p j q", q=QT)[:, 2 * jj:2 * jj + 2, qt]
                a = SM + 2 * (n % 2)
                nc.vector.tensor_reduce(dst, ps[:, a:a + 2, 0:s_width(qt)], AX.X, ALU.max,
                                        negate=True).then_inc(s_max, 1)

            def copy_pv(u):
                dve.wait_ge(pv_done, QT * (u + 1))
                nc.vector.tensor_copy(oT[:, u % 2, :], bank(PV)).then_inc(pv_copied, 1)

            def task(kind, arg):
                m = number[kind, arg]
                if kind in ("on_turn", "wo"):
                    return
                dve.wait_ge(misc_full, m + 1)
                src = bank(MISC)
                if kind == "max_t":
                    if arg >= 2:
                        dve.wait_ge(m_placed[(arg - 2) % QRING], 16 * ((arg - 2) // QRING + 1))
                    nc.vector.tensor_copy(mT[:, arg % 2, :], src[0:4 * QT, 0:P]).then_inc(m_turned, 1)
                    dve.wait_ge(m_turned, arg + 1)
                    dve.sem_inc(misc_empty, 1)
                elif kind == "affinity":
                    nc.vector.tensor_copy(aff.rearrange("p c e -> p (c e)"), src[:, 0:NT * E]).then_inc(misc_empty, 1)
                    dve.wait_ge(misc_empty, m + 1)
                    link(nc.vector.tensor_reduce(amax[:], aff[:], AX.X, ALU.max))
                    nc.vector.engine_nop().then_inc(amax_done, 1)
                    link(nc.vector.tensor_tensor(aff[:], aff[:], amax.unsqueeze(2).broadcast_to([P, NT, E]), ALU.is_equal))
                    dve.wait_ge(consts_set, 6)
                    link(nc.vector.tensor_tensor(aff[:], aff[:], firstw.unsqueeze(1).broadcast_to([P, NT, E]), ALU.mult))
                    link(nc.vector.tensor_reduce(slotf[:], aff[:], AX.X, ALU.max))
                    link(nc.vector.tensor_tensor(oneh.rearrange("p e c -> p c e"), aff[:],
                                                 slotf.unsqueeze(2).broadcast_to([P, NT, E]), ALU.is_equal))
                    nc.vector.tensor_reduce(npad_f[:], oneh[:], AX.X, ALU.add).then_inc(route, 1)
                    steps[0] += 1
                    dve.wait_ge(route, steps[0])
                    nc.vector.tensor_copy(rowtot[:], npad_f[:]).then_inc(rowtot_done, 1)
                    link(nc.vector.tensor_tensor_scan(scan.rearrange("p e c -> p (e c)"), oneF[:],
                                                      oneh.rearrange("p e c -> p (e c)"), 0.0, ALU.mult, ALU.add))
                elif kind == "prefix":
                    nc.vector.tensor_copy(pre[:], src[:, 0:2 * E]).then_inc(misc_empty, 1)
                    dve.wait_ge(misc_empty, m + 1)
                    link(nc.vector.tensor_scalar(npad_i[:], pre[:, E:2 * E], float(P - 1), None, ALU.add))
                    link(nc.vector.tensor_scalar(npad_j[:], npad_i[:], 7, 7, ALU.logical_shift_right,
                                                 ALU.logical_shift_left))
                    link(nc.vector.tensor_copy(npad[:], npad_j[:]))
                    link(nc.vector.tensor_tensor_scan(ends[:], oneF[:, 0:E], npad[:], 0.0, ALU.mult, ALU.add))
                    link(nc.vector.tensor_tensor(offs[:], ends[:], npad[:], ALU.subtract))
                    link(nc.vector.tensor_tensor(offs[:], offs[:], pre[:, 0:E], ALU.add))
                    link(nc.vector.tensor_tensor(offs[:, 1:E], offs[:, 1:E], scan[:, 0:E - 1, NT - 1], ALU.subtract))
                    link(nc.vector.tensor_tensor(scan[:], scan[:], offs.unsqueeze(2).broadcast_to([P, E, NT]), ALU.add))
                    link(nc.vector.tensor_tensor(scan[:], scan[:], oneh[:], ALU.mult))
                    link(nc.vector.tensor_reduce(slotf[:], scan.rearrange("p e c -> p c e"), AX.X, ALU.add))
                    nc.vector.tensor_scalar(slot[:], slotf[:], -1.0, None, ALU.add).then_inc(slots_done, 1)
                    link(nc.vector.tensor_tensor(starts[:], starts[:], ends[0:1, :].unsqueeze(1).broadcast_to([1, NX, E]),
                                                 ALU.is_ge))
                    link(nc.vector.tensor_reduce(expf[:], starts[:], AX.X, ALU.add))
                    nc.vector.tensor_scalar(expert[:], expf[:], float(E - 1), None, ALU.min).then_inc(experts_done, 1)
                    dve.wait_ge(ea_done, 1)
                    link(nc.vector.tensor_scalar(ea[:], ea[:], 1.0, None, ALU.add))
                    nc.vector.reciprocal(alpha[:], ea[:]).then_inc(alpha_done, 1)
                elif kind == "bias1":
                    wb = wall[:, :, O_B1:O_W2]
                    nc.vector.tensor_tensor(wb, wb, src[:, 0:E * FC].rearrange("p (e c) -> p e c", c=FC),
                                            ALU.add).then_inc(b1_done, 1)
                    dve.wait_ge(b1_done, 1)
                    dve.sem_inc(misc_empty, 1)
                elif kind in ("q_proj", "k_proj"):
                    which = 0 if kind == "q_proj" else 1
                    low_part(arg, which, src).then_inc(lo_done, 1)
                    dve.wait_ge(lo_done, 2 * arg + which + 1)
                    dve.sem_inc(misc_empty, 1)
                elif kind == "o_turn":
                    b, g = arg // G, arg % G
                    t4 = src.rearrange("p (q j w) -> p q j w", j=4, w=32)
                    nc.vector.reciprocal(rden[:, arg % 2, :, :], t4[:, :, :, DH]).then_inc(rden_done, 1)
                    dve.wait_ge(rden_done, arg + 1)
                    if g == 0 and b >= 1:
                        dve.wait_ge(misc_full, number["on_turn", b - 1] + 1)
                    dst = on[:, :, 32 * g:32 * g + 32].rearrange("p q (j d) -> p q j d", d=DH)
                    nc.vector.tensor_tensor(dst, t4[:, :, :, 0:DH],
                                            rden[:, arg % 2, :, :].unsqueeze(3).broadcast_to([P, QT, 4, DH]),
                                            ALU.mult).then_inc(o_normed, 1)
                    dve.wait_ge(o_normed, arg + 1)
                    dve.sem_inc(misc_empty, 1)

            def expert_of(j):
                return dve.value_load(expert[0:1, bass.ds(j, 1)], min_val=0, max_val=E - 1)

            def stage_1(e, par):
                nc.vector.tensor_copy(stage1[par], wall_flat[:, bass.ds(e * WW, ST1)]).then_inc(w1_staged, 1)

            def stage_2(e, par):
                nc.vector.tensor_copy(stage2[par], wall_flat[:, bass.ds(e * WW + O_W2, ST2)]).then_inc(w2_staged, 1)

            def relu_half(j, par):
                dve.wait_ge(h_full, j + 1)
                for c in range(FC // 2):
                    last = nc.vector.tensor_scalar(hid[par][:, P * c:P * (c + 1)], ps[:, 2 * par, P * c:P * (c + 1)],
                                                   stage1[par][:, F + c:F + c + 1], 0.0, ALU.add, ALU.max)
                last.then_inc(h_dve, 1)

            def copy_y(j, par):
                dve.wait_ge(y_full, j + 1)
                if not isinstance(j, int):
                    dve.wait_ge(y_sent[par], 8 * (j - par))
                elif j >= 2:
                    dve.wait_ge(y_sent[par], 16 * (j // 2))
                nc.vector.tensor_tensor(ysb[:, par, :], ps[:, 4 + par, 0:P], stage2[par][:, W2W:W2W + D],
                                        ALU.add).then_inc(y_copied, 1)

            def first_half(j, par):
                e = expert_of(j + 2)
                relu_half(j, par)
                dve.wait_ge(h_act, j + 1)
                dve.wait_ge(h_dve, j + 1)
                stage_1(e, par)

            def second_half(j, par):
                e = expert_of(j + 2)
                copy_y(j, par)
                dve.wait_ge(y_copied, j + 1)
                stage_2(e, par)

            def feed_forward():
                for n in range(0, TURNS, 2):
                    dve.wait_ge(z_turned, n + 1)
                    w = P * (min(4 * n + 4, NS) - 4 * n)
                    nc.vector.tensor_copy(zT[:, 4 * P * n:4 * P * n + w], ps[:, n, 0:w]).then_inc(zT_dve, 1)
                dve.wait_ge(z_turned, TURNS)
                dve.wait_ge(dest_copied, 1)
                dve.wait_ge(experts_done, 1)
                for j in range(2):
                    stage_1(expert_of(j), j)
                    stage_2(expert_of(j), j)
                first_half(0, 0)
                first_half(1, 1)
                second_half(0, 0)
                first_half(2, 0)
                second_half(1, 1)
                with dve.Fori(1, NS // 2) as i:
                    first_half(2 * i + 1, 1)
                    second_half(2 * i, 0)
                    first_half(2 * i + 2, 0)
                    second_half(2 * i + 1, 1)
                copy_y(NS - 1, (NS - 1) % 2)

            nc.vector.memset(oneF[:], 1.0).then_inc(consts_set, 1)
            nc.vector.memset(ones_b[:], 1.0).then_inc(consts_set, 1)
            nc.vector.memset(vp[:], 1.0).then_inc(vp_set, 1)
            for b in range(B):
                dve.wait_ge(x_in[b], 16)
                moments(b, xn, stats, mv).then_inc(var_done, 1)
                if b == 0:
                    norm(0)
                    copy_xT(0)
                    low_part(0, 0, bank(4)).then_inc(lo_done, 1)
                    low_part(0, 1, bank(5)).then_inc(lo_done, 1)
            for b in range(1, B):
                norm(b)
                copy_xT(b)
            for n in range(2 * BASE0):
                maxima(n)
            for kind, arg in tasks_at(-1):
                task(kind, arg)
            for t in range(END + 1):
                if t == FFN_AT:
                    feed_forward()
                more = t < STEPS - 2 * QT
                if more:
                    maxima(2 * BASE0 + 2 * t)
                u, kt = divmod(t, QT)
                if kt == 2 and 1 <= u <= UNITS:
                    copy_pv(u - 1)
                if t >= 1:
                    for kind, arg in tasks_at(t - 1):
                        task(kind, arg)
                if more:
                    maxima(2 * BASE0 + 2 * t + 1)
                if 2 <= t < 2 + B:
                    moments(t - 2, xn, stats, mv2).then_inc(var2_done, 1)
                if 4 <= t < 4 + B:
                    dve.wait_ge(rstd2_done, t - 3)
                    for c in range(QT * (t - 4), QT * (t - 3)):
                        last = nc.vector.tensor_scalar(zrow[:, c, 0:D], xn[:, c, :], mv2[:, c, 0:1],
                                                       rstd2[:, c:c + 1], ALU.subtract, ALU.mult)
                    last.then_inc(z_done, 1)
                if 8 <= t < 8 + E:
                    w = wall[:, t - 8, 0:F]
                    if t == 8:
                        dve.wait_ge(b1_done, 1)
                    nc.vector.tensor_scalar(w, w, lng[:, t - 8:t - 7], None, ALU.mult).then_inc(w1_folded, 1)
                for b in range(B):
                    if t == gate_at(b) + 1:
                        dve.wait_ge(gate_plus, b + 1)
                        nc.vector.reciprocal(gtmp[:, b % 2, :], gtmp[:, b % 2, :]).then_inc(gate_rec, 1)

        @block.scalar
        def _(act):
            def values(b):
                act.wait_ge(v_full, b + 1)
                if b == 0:
                    act.wait_ge(vp_set, 1)
                o = QT * b * H * VW
                dst = vp[:, o:o + QT * H * VW].rearrange("p (c h w) -> p c h w", h=H, w=VW)
                src = ps[:, 6 + b % 2, :].rearrange("p (c h w) -> p c h w", h=H, w=DH)
                for c in range(QT):
                    last = nc.scalar.activation(dst[:, c, :, 0:DH], src[:, c, :, :], ACT.Copy)
                last.then_inc(v_done, 1)

            def high_part(b, which, src):
                if b >= 1 and which == 0:
                    pair, nr = 2 * b - 1, QRING // 2
                    for q in (pair - 1, pair):
                        act.wait_ge(q_placed[q % nr], 16 * 12 * (q // nr + 1))
                if b >= 1 and which == 1:
                    act.wait_ge(k_placed[(b - 1) % 2], 16 * 3 * ((b - 1) // 2 + 1))
                nc.scalar.activation((qhl, khl)[which][:, 0, :], src, ACT.Copy).then_inc(hi_done, 1)

            def exponentials(t, j):
                u, kt = divmod(t, QT)
                lo, hi = q_tiles(kt)
                n = 4 * t + j
                act.wait_ge(st_full, n + 1)
                if j == 0 and t >= RING:
                    act.wait_ge(pv_done, t - RING + 1)
                nc.scalar.activation(probs[:, t % RING, j, 0:P * (hi - lo)], ps[:, ST + n % 2, 0:P * (hi - lo)],
                                     ACT.Exp, scale=SCALE).then_inc(exp_done, 1)

            def task(kind, arg):
                m = number[kind, arg]
                src = bank(MISC)
                if kind in ("q_proj", "k_proj"):
                    act.wait_ge(misc_full, m + 1)
                    high_part(arg, 0 if kind == "q_proj" else 1, src)
                elif kind == "on_turn":
                    act.wait_ge(misc_full, m + 1)
                    if arg >= 1:
                        act.wait_ge(misc_full, number["wo", arg - 1] + 1)
                    nc.scalar.activation(onT[:], src, ACT.Copy).then_inc(on_turned, 1)
                    act.wait_ge(on_turned, arg + 1)
                    act.sem_inc(misc_empty, 1)
                elif kind == "wo":
                    act.wait_ge(misc_full, m + 1)
                    nc.scalar.activation(s_of[arg],
                                         src.rearrange("p (c d) -> p c d", d=D), ACT.Copy).then_inc(s_ready, 1)
                    act.wait_ge(s_ready, arg + 1)
                    act.sem_inc(misc_empty, 1)

            def relu_half(j, par):
                act.wait_ge(h_full, j + 1)
                for c in range(FC // 2):
                    cc = c + FC // 2
                    last = nc.scalar.activation(hid[par][:, P * cc:P * (cc + 1)], ps[:, 2 * par + 1, P * c:P * (c + 1)],
                                                ACT.Relu, bias=stage1[par][:, F + cc:F + cc + 1])
                last.then_inc(h_act, 1)

            act.wait_ge(qk0_full, 1)
            high_part(0, 0, bank(4))
            act.wait_ge(qk0_full, 2)
            high_part(0, 1, bank(5))
            for b in range(B):
                values(b)
            for t in range(END + 1):
                if t == FFN_AT:
                    for n in range(1, TURNS, 2):
                        act.wait_ge(z_turned, n + 1)
                        w = P * (min(4 * n + 4, NS) - 4 * n)
                        nc.scalar.activation(zT[:, 4 * P * n:4 * P * n + w], ps[:, n, 0:w], ACT.Copy
                                             ).then_inc(zT_act, 1)
                    relu_half(0, 0)
                    with act.Fori(0, (NS - 1) // 2) as i:
                        relu_half(2 * i + 1, 1)
                        relu_half(2 * i + 2, 0)
                if t < STEPS:
                    exponentials(t, 0)
                    exponentials(t, 1)
                if t >= 1:
                    for kind, arg in tasks_at(t - 1):
                        task(kind, arg)
                if t == 2:
                    act.wait_ge(amax_done, 1)
                    nc.scalar.activation(ea[:], amax[:], ACT.Exp, scale=-1.0).then_inc(ea_done, 1)
                if t < STEPS:
                    exponentials(t, 2)
                    exponentials(t, 3)
                for b in range(B):
                    if t == gate_at(b):
                        act.wait_ge(gate_in, b + 1)
                        nc.scalar.activation(gtmp[:, b % 2, :].rearrange("p (c d) -> p c d", d=D),
                                             zrow[:, QT * b:QT * (b + 1), 0:D], ACT.Exp, scale=-1.0
                                             ).then_inc(gate_exp, 1)

        @block.gpsimd
        def _(pool):
            steps = [0]

            def link(ins):
                steps[0] += 1
                ins.then_inc(pool_step, 1)
                pool.wait_ge(pool_step, steps[0])

            def rsqrt(b, m, v, r, done):
                c = slice(QT * b, QT * (b + 1))
                link(nc.gpsimd.tensor_scalar(v[:, c], m[:, c, 1], EPS, None, ALU.add))
                nc.gpsimd.tensor_tensor(r[:, c], v[:, c], mhalf[:, c], ALU.pow).then_inc(done, 1)

            def mask(t):
                u, kt = divmod(t, QT)
                lo, hi = q_tiles(kt)
                pool.wait_ge(exp_done, 4 * t + 4)
                w = P * (hi - lo)
                last = None
                if kt > 0:
                    v = probs[:, t % RING, :, 0:P]
                    last = nc.gpsimd.affine_select(out=v, in_=v, compare_op=ALU.is_ge, fill=0.0, base=0,
                                                   pattern=[[0, 4], [1, P]], channel_multiplier=-1)
                    if kt == QT - 1:
                        last.then_inc(p_masked, 1)
                if kt < QT - 1:
                    v = probs[:, t % RING, :, w - P:w]
                    nc.gpsimd.affine_select(out=v, in_=v, compare_op=ALU.is_ge, fill=0.0, base=0,
                                            pattern=[[0, 4], [-1, P]], channel_multiplier=1).then_inc(p_masked, 1)

            def send_y(j, par):
                if not isinstance(j, int):
                    pool.wait_ge(y_sent[par], 8 * (j - par))
                elif j >= 2:
                    pool.wait_ge(y_sent[par], 16 * (j // 2))
                nc.gpsimd.tensor_copy(dest1[:, par, :], dest[:, bass.ds(j, 1)]).then_inc(dest_staged, 1)
                pool.wait_ge(dest_staged, j + 1)
                pool.wait_ge(y_copied, j + 1)
                pool.sem_inc(sending, 1)
                nc.gpsimd.indirect_dma_start(
                    out=f_dram, out_offset=bass.IndirectOffsetOnAxis(ap=dest1[:, par, :].bitcast(U32), axis=0),
                    in_=ysb[:, par, :], in_offset=None).then_inc(y_sent[par], 16)

            def feed_forward():
                send_y(0, 0)
                send_y(1, 1)
                with pool.Fori(1, NS // 2) as i:
                    send_y(2 * i, 0)
                    send_y(2 * i + 1, 1)
                send_y(NS - 1, (NS - 1) % 2)

            nc.gpsimd.memset(mhalf[:], -0.5).then_inc(pool_step, 1)
            steps[0] += 1
            pool.wait_ge(pool_step, steps[0])
            for r in range(QRING // 2):
                nc.gpsimd.memset(raw(qst[:, 2 * r:2 * r + 2, :, :]), 0.0).then_inc(qst_zero, 1)
                if r == 0:
                    pool.wait_ge(var_done, 1)
                    rsqrt(0, mv, vare, rstd, rstd_done)
            for b in range(1, B):
                pool.wait_ge(var_done, b + 1)
                rsqrt(b, mv, vare, rstd, rstd_done)
            pool.wait_ge(rstd_done, B)
            nc.gpsimd.memset(raw(kst[96:97, :, :, :]), 1.0).then_inc(kst_ones, 1)
            pool.wait_ge(kst_ones, 1)
            link(nc.gpsimd.memset(before[:], 1.0))
            nc.gpsimd.affine_select(out=before[:], in_=before[:], compare_op=ALU.is_gt, fill=0.0, base=0,
                                    pattern=[[1, P]], channel_multiplier=-1).then_inc(consts_set, 1)
            nc.gpsimd.iota(firstw[:], [[-1, E]], base=E, channel_multiplier=0,
                           allow_small_or_imprecise_dtypes=True).then_inc(consts_set, 1)
            pool.wait_ge(consts_set, 4)
            nc.gpsimd.iota(starts[:], [[P, NX], [0, E]], base=0, channel_multiplier=0,
                           allow_small_or_imprecise_dtypes=True).then_inc(consts_set, 1)
            pool.wait_ge(consts_set, 5)
            nc.gpsimd.iota(zrow[:, :, D:ROW].bitcast(I32), [[P, NT], [0, 1]], base=0, channel_multiplier=1
                           ).then_inc(consts_set, 1)
            nc.gpsimd.memset(zs[:, :, 0:D], 0.0).then_inc(pre_made, 1)
            nc.gpsimd.iota(zs[:, :, D:ROW].bitcast(I32), [[P, NS], [0, 1]], base=T, channel_multiplier=1
                           ).then_inc(pre_made, 1)
            for t in range(END + 1):
                if t < STEPS:
                    if t == FFN_AT:
                        feed_forward()
                    mask(t)
                if 3 <= t < 3 + B:
                    b = t - 3
                    pool.wait_ge(var2_done, b + 1)
                    rsqrt(b, mv2, vare, rstd2, rstd2_done)
                if 7 <= t < 15:
                    if t == 7:
                        pool.wait_ge(slots_done, 1)
                        pool.wait_ge(z_done, B)
                        pool.wait_ge(z_cleared, 16)
                        pool.wait_ge(consts_set, 6)
                    for c in range(2 * (t - 7), 2 * (t - 7) + 2):
                        nc.gpsimd.indirect_dma_start(
                            out=z_dram, out_offset=bass.IndirectOffsetOnAxis(ap=slot[:, c:c + 1].bitcast(U32), axis=0),
                            in_=zrow[:, c, :], in_offset=None).then_inc(z_sent, 16)
                if t == FFN_AT - 3:
                    pool.wait_ge(zs_in, 16)
                    nc.gpsimd.tensor_copy(dest[:].unsqueeze(2), zs[:, :, D:ROW].bitcast(I32)).then_inc(dest_copied, 1)
                    pool.wait_ge(dest_copied, 1)
                for b in range(B):
                    zb = zrow[:, QT * b:QT * (b + 1), 0:D]
                    gt = gtmp[:, b % 2, :].rearrange("p (c d) -> p c d", d=D)
                    if t == gate_at(b) - 1:
                        pool.wait_ge(f_in[b], 16)
                        pool.wait_ge(alpha_done, 1)
                        al = alpha[:, QT * b:QT * (b + 1)].unsqueeze(2).broadcast_to([P, QT, D])
                        link(nc.gpsimd.tensor_tensor(zb, zb, al, ALU.mult))
                        nc.gpsimd.tensor_tensor(zb, zb, xn[:, QT * b:QT * (b + 1), :], ALU.add).then_inc(gate_in, 1)
                    if t == gate_at(b):
                        pool.wait_ge(gate_exp, b + 1)
                        nc.gpsimd.tensor_scalar(gtmp[:, b % 2, :], gtmp[:, b % 2, :], 1.0, None, ALU.add
                                                ).then_inc(gate_plus, 1)
                    if t == gate_at(b) + 2:
                        pool.wait_ge(gate_rec, b + 1)
                        nc.gpsimd.tensor_tensor(zb, zb, gt, ALU.mult).then_inc(gate_done, 1)
                        pool.wait_ge(gate_done, b + 1)
                        pool.dma_start(xn[:, QT * b:QT * (b + 1), :], x_tok[:, QT * b:QT * (b + 1), :]
                                       ).then_inc(x_again[b], 16)
                    wo_at = [tt for tt, k, a in tasks if (k, a) == ("wo", b)][0]
                    if t == max(wo_at + 2, gate_at(b) + 4) or (t == END and wo_at + 2 > END):
                        pool.wait_ge(s_ready, b + 1)
                        pool.wait_ge(x_again[b], 16)
                        sv = s_of[b]
                        link(nc.gpsimd.tensor_tensor(sv, sv, zb, ALU.mult))
                        nc.gpsimd.tensor_tensor(sv, sv, xn[:, QT * b:QT * (b + 1), :], ALU.add).then_inc(res_done, 1)


_INS = ["x", "w_attn", "small", "w_ffn", "b2", "ident_in"]


def kernel(**inputs):
    import numpy as np
    import concourse.bacc as bacc
    from concourse.bass_utils import run_bass_kernel_spmd as run

    a = {k.split("_", 1)[1]: np.asarray(v) for k, v in inputs.items()}
    x = a["attn_x"]
    E, F, D = a["ffn_w1"].shape
    wq = a["attn_Wq"].reshape(2, 2, 4, 8, D).transpose(0, 2, 3, 1, 4).reshape(D, D)
    wk = a["attn_Wk"].reshape(4, 4, 8, D).transpose(1, 2, 0, 3).reshape(D, D)
    w1 = a["ffn_w1"].transpose(2, 0, 1)
    b1 = a["ffn_b1"].reshape(E, F // 128, 128).transpose(2, 0, 1)
    w2 = a["ffn_w2"].reshape(E, D, F // 128, 128).transpose(3, 0, 2, 1).reshape(128, E, F // 128 * D)
    laid = {
        "x": x.reshape(-1, D),
        "w_attn": np.stack([w.T for w in (wq, wk, a["attn_Wv"], a["attn_Wo"])], 1),
        "small": np.stack([a["ffn_centroids"].T, a["ffn_ln_g"].T, a["ffn_ln_b"].T], 1),
        "w_ffn": np.concatenate([w1, b1, w2], 2),
        "b2": a["ffn_b2"],
        "ident_in": np.eye(128, dtype=np.float32),
    }
    nc = bacc.Bacc("TRN2", target_bir_lowering=False, num_devices=1)
    arrays, args = {}, []
    for name in _INS:
        v = np.ascontiguousarray(laid[name])
        arrays[f"in_{name}_dram"] = v
        args.append(nc.dram_tensor(f"in_{name}_dram", v.shape, mybir.dt.from_np(v.dtype), kind="ExternalInput").ap())
    args.append(nc.dram_tensor("out_0_dram", (x.shape[0] * x.shape[1], D), F32, kind="ExternalOutput").ap())
    build(nc, *args)
    r = run(nc, [arrays], core_ids=[0])
    return r.results[0]["out_0_dram"].reshape(x.shape)
```

```python
from contextlib import ExitStack

import concourse.bass as bass
from concourse import mybir

ALU = mybir.AluOpType
ACT = mybir.ActivationFunctionType
AX = mybir.AxisListType
F32 = mybir.dt.float32
F32R = mybir.dt.float32r
BF16 = mybir.dt.bfloat16
I32 = mybir.dt.int32
U32 = mybir.dt.uint32

P = 128


def build(nc, x, w_attn, small, w_ffn, b2, ident_in, out):
    T, D = x.shape
    B = 4
    S = T // B
    NT = T // P
    QT = S // P
    DH = 8
    H = D // DH
    G = H // 4
    SCALE = DH ** -0.5
    E = b2.shape[0]
    F = 512
    FC = F // P
    EPS = 1e-5
    NS = (T - E) // P + E
    NX = NS + 2
    ROW = D + 1
    UNITS = B * G
    STEPS = UNITS * QT
    LAG = 2
    QRING = 6
    RING = 3
    VW = DH + 1
    ITEMS = 2 * 2 + 2 * 4
    PER_STEP = 3
    AHEAD = 2 * ITEMS - PER_STEP
    MAX_STEPS = (UNITS * ITEMS - AHEAD) // PER_STEP
    FFN_AT = STEPS // 2
    PREFIX_AT = 3
    SEND_AT = PREFIX_AT + 5
    W1W, B1W, W2W = F, FC, FC * D
    O_B1, O_W2, O_B2 = W1W, W1W + B1W, W1W + B1W + W2W
    WW = O_B2 + D
    ST1 = W1W + B1W
    ST2 = W2W + D

    def q_tiles(kt):
        return max(0, kt - 1), min(QT, kt + 2)

    def item_of(n):
        u, i = divmod(n, ITEMS)
        if i < 2:
            return u, 0, (2 * i, 2 * i + 1)
        if i >= ITEMS - 2:
            i -= ITEMS - 2
            return u, QT - 1, (2 * i, 2 * i + 1)
        return u, 1 + (i - 2) // 4, ((i - 2) % 4,)

    def first_item(t):
        return AHEAD + PER_STEP * t

    tasks = []
    for t in range(-1, STEPS + 8):
        u, kt = divmod(t, QT)
        g, b = u % G, u // G
        if t == -1:
            tasks += [(t, "affinity", 0), (t, "aff_turn", 0), (t, "max_t", 0)]
            continue
        if t == PREFIX_AT:
            tasks.append((t, "prefix", 0))
        if kt == 1 and u + 1 < UNITS:
            tasks.append((t, "max_t", u + 1))
        if kt == 0 and g == 0 and b + 1 < B:
            tasks.append((t, "q_proj", b + 1))
        if kt == 2 and g == 0 and b + 1 < B:
            tasks.append((t, "k_proj", b + 1))
        if kt == 3 and 1 <= u <= UNITS:
            tasks.append((t, "o_turn", u - 1))
        if kt == 0 and g == 1 and b >= 1:
            tasks.append((t, "on_turn", b - 1))
        if kt == 2 and g == 1 and b >= 1:
            tasks.append((t, "wo", b - 1))
    TURNS = (NS + 3) // 4
    assert TURNS == 6 and len({t for t, _, _ in tasks if t >= 0}) == len(tasks) - 3
    number = {(kind, arg): m for m, (_, kind, arg) in enumerate(tasks)}
    END = max(t for t, _, _ in tasks) + 1

    def emptied(kind, arg):
        return number[kind, arg] + 1

    def tasks_at(t):
        return [(kind, arg) for at, kind, arg in tasks if at == t]

    with ExitStack() as ctx:
        def sb(name, shape, dt=F32):
            return ctx.enter_context(nc.sbuf_tensor(name, shape, dt)).ap()

        def sem(name):
            return ctx.enter_context(nc.semaphore(name))

        ident = sb("ident", [P, P])
        before = sb("before", [P, P], BF16)
        ones_b = sb("ones_b", [P, P], BF16)
        xn = sb("xn", [P, NT, D])
        zrow = sb("zrow", [P, NT, ROW])
        xnT = sb("xnT", [P, T])
        wqk = sb("wqk", [P, 4, D])
        features = sb("features", [P, 4, E])
        cent32 = features.rearrange("p n e -> p (n e)")
        lng, lnb = features[:, 1, :], features[:, 2, :]
        wall = sb("wall", [P, E, WW])
        wall_flat = wall.rearrange("p e w -> p (e w)")
        vp = sb("vp", [P, NT * H * VW + 32 - VW])
        qhl = sb("qhl", [P, 2, S], F32R)
        khl = sb("khl", [P, 2, S], F32R)
        qst = sb("qst", [P, QRING, 4, S], F32R)
        kst = sb("kst", [P, 2, G, S], F32R)
        mneg = sb("mneg", [P, 2, 4 * QT])
        mT = sb("mT", [4 * QT, 2, P], F32R)
        probs = sb("probs", [P, RING, 4, 3 * P])
        oT = sb("oT", [P, 2, S])
        rden = sb("rden", [P, 2, QT, 4])
        on = sb("on", [P, QT, D])
        onT = sb("onT", [P, S])
        s0 = sb("s0", [P, QT, D])
        gtmp = sb("gtmp", [P, 2, QT * D])
        stats = sb("stats", [P, NT, 6])
        mv = sb("mv", [P, NT, 2])
        vare = sb("vare", [P, NT])
        rstd = sb("rstd", [P, NT])
        mv2 = sb("mv2", [P, NT, 2])
        rstd2 = sb("rstd2", [P, NT])
        shift2 = mv[:, :, 0]
        mhalf = sb("mhalf", [P, NT])
        pool_ws = sb("pool_ws", [P, 2 * ST1 + 2 * ST2 + 2 * F])
        zs = pool_ws[:, 0:NS * ROW].rearrange("p (j r) -> p j r", r=ROW)
        o = 0
        stage1, stage2, hid = [], [], []
        for par in range(2):
            stage1.append(pool_ws[:, o:o + ST1])
            o += ST1
        for par in range(2):
            stage2.append(pool_ws[:, o:o + ST2])
            o += ST2
        for par in range(2):
            hid.append(pool_ws[:, o:o + F])
            o += F
        zT = sb("zT", [P, NS * P])
        s_of = [s0] + [zT[:, S * (b - 1):S * b].rearrange("p (c d) -> p c d", d=D) for b in range(1, B)]
        dest = sb("dest", [P, NS], I32)
        dest1 = sb("dest1", [P, 2, 1], I32)
        ysb = sb("ysb", [P, 2, D])
        aff = sb("aff", [P, NT, E])
        amax = sb("amax", [P, NT])
        alpha = sb("alpha", [P, NT])
        ea = sb("ea", [P, NT])
        firstw = sb("firstw", [P, E])
        oneh = sb("oneh", [P, E, NT])
        rowtot = sb("rowtot", [P, E], BF16)
        oneF = sb("oneF", [P, E * NT])
        scan = sb("scan", [P, E, NT])
        pre = sb("pre", [P, 2 * E])
        npad_f = sb("npad_f", [P, E])
        npad_i = sb("npad_i", [P, E], I32)
        npad_j = sb("npad_j", [P, E], I32)
        npad = sb("npad", [P, E])
        ends = sb("ends", [P, E])
        offs = sb("offs", [P, E])
        slotf = sb("slotf", [P, NT])
        slot = sb("slot", [P, NT], I32)
        starts = sb("starts", [P, NX, E])
        expf = sb("expf", [P, NX])
        tile_gain = aff.rearrange("p c e -> p (c e)")[:, 0:NS]
        tile_bias = aff.rearrange("p c e -> p (c e)")[:, NS:2 * NS]
        expert = sb("expert", [1, NX], I32)
        ps = ctx.enter_context(nc.psum_tensor("ps", [P, 8, 512], F32))
        ST, SM, PV, MISC = 0, 3, 6, 7
        RINGS = SM - ST

        z_dram = nc.dram_tensor("z_dram", (NS * P, ROW), F32, kind="Internal").ap()
        f_dram = nc.dram_tensor("f_dram", (T + NS * P, D), F32, kind="Internal").ap()

        x_in = [sem(f"x_in{b}") for b in range(B)]
        ident_in_s = sem("ident_in_s")
        proj_in = sem("proj_in")
        small_in = sem("small_in")
        w_in = sem("w_in")
        consts_set = sem("consts_set")
        vp_set = sem("vp_set")
        qst_zero = sem("qst_zero")
        kst_ones = sem("kst_ones")
        var_done = sem("var_done")
        rstd_done = sem("rstd_done")
        xn_done = sem("xn_done")
        stat_step = sem("stat_step")
        xnT_full = sem("xnT_full")
        xnT_done = sem("xnT_done")
        v_full = sem("v_full")
        v_done = sem("v_done")
        qk0_full = sem("qk0_full")
        hi_done = sem("hi_done")
        lo_done = sem("lo_done")
        q_placed = [sem(f"q_placed{r}") for r in range(QRING // 2)]
        first_k_placed = sem("first_k_placed")
        k_placed = [sem(f"k_placed{r}") for r in range(2)]
        s_full = sem("s_full")
        s_max = sem("s_max")
        m_placed = [sem(f"m_placed{r}") for r in range(QRING)]
        st_full = sem("st_full")
        exp_done = sem("exp_done")
        p_masked = sem("p_masked")
        pv_done = sem("pv_done")
        pv_copied = sem("pv_copied")
        misc_full = sem("misc_full")
        misc_empty = sem("misc_empty")
        rden_done = sem("rden_done")
        amax_done = sem("amax_done")
        ea_done = sem("ea_done")
        alpha_done = sem("alpha_done")
        route = sem("route")
        rowtot_done = sem("rowtot_done")
        slots_done = sem("slots_done")
        experts_done = sem("experts_done")
        pre_made = sem("pre_made")
        z_cleared = sem("z_cleared")
        var2_done = sem("var2_done")
        rstd2_done = sem("rstd2_done")
        z_done = sem("z_done")
        z_sent = sem("z_sent")
        zs_in = sem("zs_in")
        dest_copied = sem("dest_copied")
        z_turned = sem("z_turned")
        zT_dve = sem("zT_dve")
        zT_act = sem("zT_act")
        gain_made = sem("gain_made")
        w1_staged = sem("w1_staged")
        w2_staged = sem("w2_staged")
        dest_staged = sem("dest_staged")
        sending = sem("sending")
        h_full = sem("h_full")
        h_dve = sem("h_dve")
        h_act = sem("h_act")
        y_full = sem("y_full")
        y_copied = sem("y_copied")
        y_sent = [sem(f"y_sent{r}") for r in range(2)]
        f_in = [sem(f"f_in{b}") for b in range(B)]
        x_again = [sem(f"x_again{b}") for b in range(B)]
        gate_in = sem("gate_in")
        gate_exp = sem("gate_exp")
        gate_rec = sem("gate_rec")
        gate_done = [sem(f"gate_done{b}") for b in range(B)]
        pool_step = sem("pool_step")
        res_done = [sem(f"res_done{b}") for b in range(B)]
        stored = sem("stored")

        def bank(n):
            return ps[:, n, :]

        def gate_at(b):
            return (FFN_AT + 4, FFN_AT + 12, MAX_STEPS - 5, MAX_STEPS - 1)[b]

        def reciprocal_at(b):
            return gate_at(b) + 2 if b in ON_POOL else MAX_STEPS + QT * (b - 2)

        def silu_at(b):
            return reciprocal_at(b) + QT

        ON_POOL = (0, 1)

        ST_MORE = 4 * MAX_STEPS

        def st_bank(n):
            return ST + n % RINGS if n < ST_MORE else ST + n % (2 * RINGS)

        def raw(ap):
            return ap.bitcast(F32)

        def lhs_v(tile, h):
            o = (tile * H + h) * VW
            return vp[:, o:o + 32]

        def s_width(qt):
            lo, hi = q_tiles(qt)
            return (hi - lo) * P

        K_HI, K_LO = [(0, 0), (2, 0)], [(1, 1)]

        def k_placed_in(b):
            return (first_k_placed, 16 * 3) if b == 0 else (k_placed[b % 2], 16 * 3 * ((b + 1) // 2))

        def k_slots(engine, b, slots):
            for slot_n, part in slots:
                engine.dma_start(raw(kst[32 * slot_n:32 * slot_n + 32, b % 2, :, :]),
                                 raw(khl[:, part, :])).then_inc(k_placed_in(b)[0], 16)

        x_tok = x.rearrange("(c p) d -> p c d", p=P)
        out_tok = out.rearrange("(c p) d -> p c d", p=P)
        f_tok = f_dram[0:T, :].rearrange("(c p) d -> p c d", p=P)

        block = ctx.enter_context(nc.Block())

        @block.sync
        def _(sp):
            def load_x(b):
                sp.dma_start(xn[:, QT * b:QT * (b + 1), :], x_tok[:, QT * b:QT * (b + 1), :]).then_inc(x_in[b], 16)

            load_x(0)
            sp.dma_start(ident[:], ident_in).then_inc(ident_in_s, 16)
            sp.dma_start(wqk, w_attn).then_inc(proj_in, 16)
            for b in range(1, B):
                load_x(b)
            sp.dma_start(features, small).then_inc(small_in, 16)

            def load_x_again(b):
                sp.dma_start(xn[:, QT * b:QT * (b + 1), :], x_tok[:, QT * b:QT * (b + 1), :]).then_inc(x_again[b], 16)

            def q_slots(pair, slots):
                half, r = pair % 2, 2 * pair % QRING
                for slot_n, part in slots:
                    for j in range(4):
                        sp.dma_start(raw(qst[32 * slot_n + 8 * j:32 * slot_n + 8 * j + 8, r:r + 2, j, :]),
                                     raw(qhl[64 * half + 16 * j:64 * half + 16 * j + 16, part, :])
                                     ).then_inc(q_placed[pair % (QRING // 2)], 16)

            Q_HI, Q_LO = [(0, 0), (1, 0)], [(2, 1)]

            def place_q(pair):
                if pair < QRING // 2:
                    sp.wait_ge(qst_zero, pair + 1)
                else:
                    sp.wait_ge(st_full, 16 * (2 * pair - QRING + 2))
                if pair >= 2:
                    sp.wait_ge(misc_empty, emptied("q_proj", pair // 2))
                else:
                    sp.wait_ge(lo_done, 1)
                q_slots(pair, Q_HI + Q_LO)

            def place_k(b):
                sp.wait_ge(misc_empty, emptied("k_proj", b))
                if b >= 2:
                    sp.wait_ge(st_full, 16 * G * (b - 1))
                k_slots(sp, b, K_HI + K_LO)

            def place_m(u):
                sp.wait_ge(misc_empty, emptied("max_t", u))
                if u >= QRING:
                    sp.wait_ge(st_full, 16 * (u - QRING + 1))
                sp.dma_start(raw(qst[96:97, u % QRING, :, :]), raw(mT[:, u % 2, :])).then_inc(m_placed[u % QRING], 16)

            sp.wait_ge(qst_zero, 1)
            sp.wait_ge(hi_done, 1)
            q_slots(0, Q_HI)
            sp.wait_ge(lo_done, 1)
            q_slots(0, Q_LO)
            place_q(1)
            place_m(0)
            sp.wait_ge(pre_made, 2)
            sp.dma_start(z_dram.rearrange("(j p) r -> p j r", p=P), zs).then_inc(z_cleared, 16)
            place_m(1)
            for u in range(UNITS):
                if u % 2 == 0 and u + 4 < UNITS:
                    place_q(u // 2 + 2)
                if u == E - 1:
                    sp.dma_start(wall[:, :, O_B2:WW], b2.partition_broadcast(P)).then_inc(w_in, 16)
                if u < E:
                    sp.dma_start(wall[:, u, 0:O_B2], w_ffn[:, u, :]).then_inc(w_in, 16)
                if u + 2 < UNITS:
                    place_m(u + 2)
                if u % G == 0 and u + G < UNITS:
                    place_k(u // G + 1)
                if u == (SEND_AT + NT) // QT - 1:
                    sp.wait_ge(z_sent, 16 * NT)
                    sp.dma_start(zs, z_dram.rearrange("(j p) r -> p j r", p=P)).then_inc(zs_in, 16)
                for b in range(B):
                    if u == min(silu_at(b) // QT, UNITS) - 1:
                        sp.wait_ge(gate_in, b + 1)
                        load_x_again(b)
                if u == FFN_AT // QT - 1:
                    sp.wait_ge(y_sent[0], 16 * ((NS + 1) // 2))
                    sp.wait_ge(y_sent[1], 16 * (NS // 2))
                    for c in range(B):
                        sp.dma_start(zrow[:, QT * c:QT * (c + 1), 0:D], f_tok[:, QT * c:QT * (c + 1), :]
                                     ).then_inc(f_in[c], 16)
            for b in range(B):
                sp.wait_ge(res_done[b], 1)
                sp.dma_start(out_tok[:, QT * b:QT * (b + 1), :], s_of[b]).then_inc(stored, 16)
            sp.wait_ge(stored, 16 * B)

        @block.tensor
        def _(pe):
            def turn_x(b):
                pe.wait_ge(xn_done, b + 1)
                for c in range(QT):
                    mm = nc.tensor.transpose(ps[:, b, P * c:P * (c + 1)], xn[:, QT * b + c, :], ident[:])
                mm.then_inc(xnT_full, 1)

            def project(dst, w, b):
                return nc.tensor.matmul(dst, wqk[:, w, :], xnT[:, S * b:S * (b + 1)], start=True, stop=True)

            def values(b):
                pe.wait_ge(xnT_done, b + 1)
                if b >= 2:
                    pe.wait_ge(v_done, b - 1)
                for c in range(QT):
                    mm = nc.tensor.matmul(ps[:, 6 + b % 2, P * c:P * (c + 1)],
                                          xnT[:, S * b + P * c:S * b + P * (c + 1)], wqk[:, 2, :],
                                          start=True, stop=True)
                mm.then_inc(v_full, 1)

            def maxima_item(n):
                u, qt, heads = item_of(n)
                b, g, r = u // G, u % G, u % QRING
                lo, hi = q_tiles(qt)
                w = P * (hi - lo)
                if n % ITEMS == 0:
                    pair, nr = u // 2, QRING // 2
                    pe.wait_ge(q_placed[pair % nr], 16 * 12 * (pair // nr + 1))
                    pe.wait_ge(*k_placed_in(b))
                if n >= RINGS:
                    pe.wait_ge(s_max, n - RINGS + 1)
                for i, j in enumerate(heads):
                    mm = nc.tensor.matmul(ps[:, SM + n % RINGS, w * i:w * (i + 1)],
                                          qst[0:96, r, j, P * qt:P * (qt + 1)],
                                          kst[0:96, b % 2, g, P * lo:P * hi], start=True, stop=True)
                mm.then_inc(s_full, 1)

            def score(t, j):
                u, kt = divmod(t, QT)
                b, g = u // G, u % G
                n = 4 * t + j
                lo, hi = q_tiles(kt)
                if n == ST_MORE:
                    pe.wait_ge(s_max, ITEMS * UNITS)
                if kt == 0 and j == 0:
                    pe.wait_ge(m_placed[u % QRING], 16 * (u // QRING + 1))
                    if u == 0:
                        pe.wait_ge(kst_ones, 1)
                if n >= RINGS:
                    ahead = RINGS if n < ST_MORE + 2 * RINGS else 2 * RINGS
                    pe.wait_ge(exp_done, n - ahead + 1)
                nc.tensor.matmul(ps[:, st_bank(n), 0:P * (hi - lo)], kst[0:97, b % 2, g, P * kt:P * (kt + 1)],
                                 qst[0:97, u % QRING, j, P * lo:P * hi], start=True, stop=True).then_inc(st_full, 1)

            def weighted(t):
                u, kt = divmod(t, QT)
                b, g = u // G, u % G
                lo, hi = q_tiles(kt)
                pe.wait_ge(p_masked, t + 1)
                if kt == 0 and u >= 1:
                    pe.wait_ge(pv_copied, u)
                for j in range(4):
                    mm = nc.tensor.matmul(ps[32 * j:32 * j + 32, PV, P * lo:P * hi],
                                          lhs_v(QT * b + kt, 4 * g + j), probs[:, t % RING, j, 0:P * (hi - lo)],
                                          start=(kt == 0), stop=(kt == QT - 1), skip_group_check=True)
                mm.then_inc(pv_done, 1)

            def task(kind, arg):
                m = number[kind, arg]
                if m >= 1:
                    pe.wait_ge(misc_empty, m)
                dst = bank(MISC)
                if kind == "max_t":
                    pe.wait_ge(s_max, ITEMS * (arg + 1))
                    mm = nc.tensor.transpose(dst[0:4 * QT, 0:P], mneg[:, arg % 2, :], ident[:])
                elif kind == "affinity":
                    pe.wait_ge(small_in, 16)
                    for b in range(B):
                        mm = nc.tensor.matmul(dst[32 * b:32 * b + 32, :], cent32, xnT[:, S * b:S * (b + 1)],
                                              start=True, stop=True, skip_group_check=True)
                elif kind == "aff_turn":
                    for qt in range(QT):
                        mm = nc.tensor.transpose(dst[:, P * qt:P * (qt + 1)], oT[:, 1, P * qt:P * (qt + 1)], ident[:])
                elif kind == "prefix":
                    pe.wait_ge(rowtot_done, 1)
                    pe.wait_ge(consts_set, 5)
                    nc.tensor.matmul(dst[:, 0:E], before[:], rowtot[:], start=True, stop=True)
                    mm = nc.tensor.matmul(dst[:, E:2 * E], ones_b[:], rowtot[:], start=True, stop=True)
                elif kind == "q_proj":
                    mm = project(dst, 0, arg)
                elif kind == "k_proj":
                    mm = project(dst, 1, arg)
                elif kind == "o_turn":
                    pe.wait_ge(pv_copied, arg + 1)
                    for qt in range(QT):
                        mm = nc.tensor.transpose(dst[:, P * qt:P * (qt + 1)], oT[:, arg % 2, P * qt:P * (qt + 1)],
                                                 ident[:])
                elif kind == "on_turn":
                    pe.wait_ge(misc_empty, emptied("o_turn", G * arg + G - 1))
                    for qt in range(QT):
                        mm = nc.tensor.transpose(dst[:, P * qt:P * (qt + 1)], on[:, qt, :], ident[:])
                elif kind == "wo":
                    pe.wait_ge(misc_empty, emptied("on_turn", arg))
                    for qt in range(QT):
                        mm = nc.tensor.matmul(dst[:, P * qt:P * (qt + 1)], onT[:, P * qt:P * (qt + 1)], wqk[:, 3, :],
                                              start=True, stop=True)
                mm.then_inc(misc_full, 1)

            def hidden(j, par):
                if isinstance(j, int) and j <= 2:
                    pe.wait_ge(zT_dve, j + 1)
                    pe.wait_ge(zT_act, j + 1)
                pe.wait_ge(w1_staged, j + 1)
                if not isinstance(j, int) or j >= 2:
                    pe.wait_ge(h_dve, j - 1)
                    pe.wait_ge(h_act, j - 1)
                for c in range(FC):
                    mm = nc.tensor.matmul(ps[:, 2 * par + c // 2, P * (c % 2):P * (c % 2) + P],
                                          stage1[par][:, P * c:P * (c + 1)], zT[:, bass.ds(j * P, P)],
                                          start=True, stop=True)
                mm.then_inc(h_full, 1)

            def output(j, par):
                pe.wait_ge(w2_staged, j + 1)
                pe.wait_ge(h_dve, j + 1)
                pe.wait_ge(h_act, j + 1)
                if not isinstance(j, int) or j >= 2:
                    pe.wait_ge(y_copied, j - 1)
                for c in range(FC):
                    mm = nc.tensor.matmul(ps[:, 4 + par, 0:P], hid[par][:, P * c:P * (c + 1)],
                                          stage2[par][:, P * c:P * (c + 1)], start=(c == 0), stop=(c == FC - 1))
                mm.then_inc(y_full, 1)

            def feed_forward():
                pe.wait_ge(exp_done, 4 * FFN_AT)
                pe.wait_ge(s_max, first_item(FFN_AT))
                pe.wait_ge(zs_in, 16)
                for n in range(TURNS):
                    for c in range(4 * n, min(4 * n + 4, NS)):
                        mm = nc.tensor.transpose(ps[:, n, P * (c % 4):P * (c % 4) + P], zs[:, c, 0:D], ident[:])
                    mm.then_inc(z_turned, 1)
                for t in range(FFN_AT - LAG, FFN_AT):
                    weighted(t)
                hidden(0, 0)
                hidden(1, 1)
                pe.wait_ge(zT_dve, TURNS // 2)
                output(0, 0)
                hidden(2, 0)
                output(1, 1)
                with pe.Fori(1, NS // 2) as i:
                    hidden(2 * i + 1, 1)
                    output(2 * i, 0)
                    hidden(2 * i + 2, 0)
                    output(2 * i + 1, 1)
                output(NS - 1, (NS - 1) % 2)
                pe.wait_ge(y_copied, NS)

            pe.wait_ge(ident_in_s, 16)
            turn_x(0)
            pe.wait_ge(xnT_done, 1)
            pe.wait_ge(proj_in, 16)
            project(bank(4), 0, 0).then_inc(qk0_full, 1)
            project(bank(5), 1, 0).then_inc(qk0_full, 1)
            values(0)
            for b in range(1, B):
                turn_x(b)
            for b in range(1, B):
                values(b)
            pe.wait_ge(xnT_done, B)
            pe.wait_ge(lo_done, 2)
            pe.wait_ge(v_done, B)
            task("affinity", 0)
            for n in range(ITEMS + 1):
                maxima_item(n)
                if n == RINGS - 1:
                    task("aff_turn", 0)
            task("max_t", 0)
            for n in range(ITEMS + 1, first_item(0)):
                maxima_item(n)
            for t in range(END):
                if t == FFN_AT:
                    feed_forward()
                more = t < MAX_STEPS
                for j in range(4):
                    if j == 3:
                        for kind, arg in tasks_at(t):
                            task(kind, arg)
                    if t < STEPS:
                        score(t, j)
                        if more and j < PER_STEP:
                            maxima_item(first_item(t) + j)
                if LAG <= t < STEPS + LAG and not FFN_AT <= t < FFN_AT + LAG:
                    weighted(t - LAG)

        @block.vector
        def _(dve):
            steps = [0]

            def link(ins):
                steps[0] += 1
                ins.then_inc(route, 1)
                dve.wait_ge(route, steps[0])

            def moments(b, src, st, m):
                for c in range(QT * b, QT * (b + 1)):
                    nc.vector.bn_stats(st[:, c, :], src[:, c, 0:D]).then_inc(stat_step, 1)
                dve.wait_ge(stat_step, stat_count(QT))
                for c in range(QT * b, QT * (b + 1)):
                    last = nc.vector.bn_aggr(m[:, c, :], st[:, c, :])
                return last

            counted = [0]

            def stat_count(n):
                counted[0] += n
                return counted[0]

            def norm(b):
                dve.wait_ge(rstd_done, b + 1)
                for c in range(QT * b, QT * (b + 1)):
                    last = nc.vector.tensor_scalar(xn[:, c, :], xn[:, c, :], mv[:, c, 0:1], rstd[:, c:c + 1],
                                                   ALU.subtract, ALU.mult)
                last.then_inc(xn_done, 1)

            def low_part(b, which, src):
                dve.wait_ge(hi_done, 2 * b + which + 1)
                hl = (qhl, khl)[which]
                return nc.vector.tensor_tensor(hl[:, 1, :], src, hl[:, 0, :].bitcast(F32), ALU.subtract)

            def maxima(n):
                u, qt, heads = item_of(n)
                dve.wait_ge(s_full, n + 1)
                if n % ITEMS == 0 and u >= 2:
                    dve.wait_ge(misc_full, number["max_t", u - 2] + 1)
                j, k, w = heads[0], len(heads), s_width(qt)
                dst = mneg[:, u % 2, :].rearrange("p (j q) -> p j q", q=QT)[:, j:j + k, qt]
                src = ps[:, SM + n % RINGS, 0:k * w].rearrange("p (j k) -> p j k", j=k)
                nc.vector.tensor_reduce(dst, src, AX.X, ALU.max, negate=True).then_inc(s_max, 1)

            def task(kind, arg):
                m = number[kind, arg]
                if kind in ("max_t", "affinity", "aff_turn", "on_turn") or (kind == "wo" and arg < B - 1):
                    return
                dve.wait_ge(misc_full, m + 1)
                src = bank(MISC)
                if kind == "prefix":
                    nc.vector.tensor_copy(pre[:], src[:, 0:2 * E]).then_inc(misc_empty, 1)
                elif kind in ("q_proj", "k_proj"):
                    which = 0 if kind == "q_proj" else 1
                    low_part(arg, which, src).then_inc(misc_empty, 1)
                elif kind == "o_turn":
                    b, g = arg // G, arg % G
                    t4 = src.rearrange("p (q j w) -> p q j w", j=4, w=32)
                    nc.vector.reciprocal(rden[:, arg % 2, :, :], t4[:, :, :, DH]).then_inc(rden_done, 1)
                    dve.wait_ge(rden_done, arg + 1)
                    if g == 0 and b >= 1:
                        dve.wait_ge(misc_full, number["on_turn", b - 1] + 1)
                    dst = on[:, :, 32 * g:32 * g + 32].rearrange("p q (j d) -> p q j d", d=DH)
                    nc.vector.tensor_tensor(dst, t4[:, :, :, 0:DH],
                                            rden[:, arg % 2, :, :].unsqueeze(3).broadcast_to([P, QT, 4, DH]),
                                            ALU.mult).then_inc(misc_empty, 1)
                elif kind == "wo":
                    dve.wait_ge(gate_done[arg], 1)
                    dve.wait_ge(x_again[arg], 16)
                    zb, sv = zrow[:, QT * arg:QT * (arg + 1), 0:D], s_of[arg]
                    nc.vector.tensor_tensor(sv, src.rearrange("p (c d) -> p c d", d=D), zb, ALU.mult
                                            ).then_inc(misc_empty, 1)
                    dve.wait_ge(misc_empty, m + 1)
                    nc.vector.tensor_tensor(sv, sv, xn[:, QT * arg:QT * (arg + 1), :], ALU.add
                                            ).then_inc(res_done[arg], 1)

            def routing(stage):
                by_expert = scan.rearrange("p e c -> p (e c)")
                if stage == 0:
                    dve.wait_ge(misc_empty, emptied("aff_turn", 0))
                    link(nc.vector.tensor_reduce(amax[:], aff[:], AX.X, ALU.max))
                    link(nc.vector.tensor_tensor(aff[:], aff[:], amax.unsqueeze(2).broadcast_to([P, NT, E]),
                                                 ALU.is_equal))
                    dve.sem_inc(amax_done, 1)
                    dve.wait_ge(consts_set, 5)
                    link(nc.vector.tensor_tensor(aff[:], aff[:], firstw.unsqueeze(1).broadcast_to([P, NT, E]),
                                                 ALU.mult))
                elif stage == 1:
                    link(nc.vector.tensor_reduce(slotf[:], aff[:], AX.X, ALU.max))
                    link(nc.vector.tensor_tensor(oneh.rearrange("p e c -> p c e"), aff[:],
                                                 slotf.unsqueeze(2).broadcast_to([P, NT, E]), ALU.is_equal))
                    link(nc.vector.tensor_reduce(npad_f[:], oneh[:], AX.X, ALU.add))
                    nc.vector.tensor_copy(rowtot[:], npad_f[:]).then_inc(rowtot_done, 1)
                elif stage == 2:
                    link(nc.vector.tensor_tensor_scan(by_expert, oneF[:], oneh.rearrange("p e c -> p (e c)"), 0.0,
                                                      ALU.mult, ALU.add))
                elif stage == 3:
                    dve.wait_ge(misc_empty, emptied("prefix", 0))
                    link(nc.vector.tensor_scalar(npad_i[:], pre[:, E:2 * E], float(P - 1), None, ALU.add))
                    link(nc.vector.tensor_scalar(npad_j[:], npad_i[:], 7, 7, ALU.logical_shift_right,
                                                 ALU.logical_shift_left))
                    link(nc.vector.tensor_copy(npad[:], npad_j[:]))
                elif stage == 4:
                    link(nc.vector.tensor_tensor_scan(ends[:], oneF[:, 0:E], npad[:], 0.0, ALU.mult, ALU.add))
                    link(nc.vector.tensor_tensor(offs[:], ends[:], npad[:], ALU.subtract))
                    link(nc.vector.tensor_tensor(offs[:], offs[:], pre[:, 0:E], ALU.add))
                elif stage == 5:
                    link(nc.vector.tensor_tensor(offs[:, 1:E], offs[:, 1:E], scan[:, 0:E - 1, NT - 1], ALU.subtract))
                    link(nc.vector.tensor_tensor(scan[:], scan[:], offs.unsqueeze(2).broadcast_to([P, E, NT]), ALU.add))
                    link(nc.vector.tensor_tensor(scan[:], scan[:], oneh[:], ALU.mult))
                elif stage == 6:
                    link(nc.vector.tensor_reduce(slotf[:], scan.rearrange("p e c -> p c e"), AX.X, ALU.add))
                    nc.vector.tensor_scalar(slot[:], slotf[:], -1.0, None, ALU.add).then_inc(slots_done, 1)
                elif stage == 7:
                    link(nc.vector.tensor_tensor(starts[:], starts[:], ends.unsqueeze(1).broadcast_to([P, NX, E]),
                                                 ALU.is_ge))
                    link(nc.vector.tensor_reduce(expf[:], starts[:], AX.X, ALU.add))
                    link(nc.vector.tensor_scalar(expf[:], expf[:], float(E - 1), None, ALU.min))
                elif stage == 8:
                    nc.vector.tensor_copy(expert[:], expf[0:1, :]).then_inc(experts_done, 1)
                    dve.wait_ge(experts_done, 1)
                    link(nc.vector.tensor_scalar(expf[:], expf[:], -1.0, float(E), ALU.mult, ALU.add))
                    link(nc.vector.tensor_tensor(starts[:], firstw.unsqueeze(1).broadcast_to([P, NX, E]),
                                                 expf.unsqueeze(2).broadcast_to([P, NX, E]), ALU.is_equal))
                elif stage in (9, 10):
                    picked = gtmp[:, 0, 0:NS * E].rearrange("p (j e) -> p j e", e=E)
                    table, of_tile = ((lng, tile_gain), (lnb, tile_bias))[stage - 9]
                    link(nc.vector.tensor_tensor(picked, starts[:, 0:NS, :],
                                                 table.unsqueeze(1).broadcast_to([P, NS, E]), ALU.mult))
                    link(nc.vector.tensor_reduce(of_tile, picked, AX.X, ALU.add))
                    dve.sem_inc(gain_made, 1)
                elif stage == 11:
                    dve.wait_ge(ea_done, 1)
                    link(nc.vector.tensor_scalar(ea[:], ea[:], 1.0, None, ALU.add))
                    nc.vector.reciprocal(alpha[:], ea[:]).then_inc(alpha_done, 1)

            def expert_of(j):
                return dve.value_load(expert[0:1, bass.ds(j, 1)], min_val=0, max_val=E - 1)

            def stage_1(e, par):
                nc.vector.tensor_copy(stage1[par], wall_flat[:, bass.ds(e * WW, ST1)]).then_inc(w1_staged, 1)

            def relu_half(j, par):
                dve.wait_ge(h_full, j + 1)
                for c in range(FC // 2):
                    last = nc.vector.tensor_scalar(hid[par][:, P * c:P * (c + 1)], ps[:, 2 * par, P * c:P * (c + 1)],
                                                   stage1[par][:, F + c:F + c + 1], 0.0, ALU.add, ALU.max)
                last.then_inc(h_dve, 1)

            def copy_y(j, par):
                dve.wait_ge(y_full, j + 1)
                if not isinstance(j, int):
                    dve.wait_ge(y_sent[par], 8 * (j - par))
                elif j >= 2:
                    dve.wait_ge(y_sent[par], 16 * (j // 2))
                nc.vector.tensor_tensor(ysb[:, par, :], ps[:, 4 + par, 0:P], stage2[par][:, W2W:W2W + D],
                                        ALU.add).then_inc(y_copied, 1)

            def slot_tile(j, par, before):
                e = expert_of(j + 2)
                relu_half(j, par)
                copy_y(before, 1 - par)
                dve.wait_ge(h_act, j + 1)
                dve.wait_ge(h_dve, j + 1)
                stage_1(e, par)

            def turned_rows(n):
                dve.wait_ge(z_turned, n + 1)
                for c in range(4 * n, min(4 * n + 4, NS)):
                    last = nc.vector.tensor_scalar(zT[:, P * c:P * (c + 1)], ps[:, n, P * (c % 4):P * (c % 4) + P],
                                                   tile_gain[:, c:c + 1], tile_bias[:, c:c + 1], ALU.mult, ALU.add)
                last.then_inc(zT_dve, 1)

            def feed_forward():
                dve.wait_ge(experts_done, 1)
                e = [expert_of(j) for j in range(2)]
                dve.wait_ge(gain_made, 2)
                turned_rows(0)
                dve.wait_ge(z_turned, TURNS)
                dve.wait_ge(dest_copied, 1)
                dve.wait_ge(w_in, 16 * (E + 1))
                stage_1(e[0], 0)
                turned_rows(2)
                stage_1(e[1], 1)
                e = expert_of(2)
                relu_half(0, 0)
                turned_rows(4)
                dve.wait_ge(h_act, 1)
                dve.wait_ge(h_dve, 1)
                stage_1(e, 0)
                slot_tile(1, 1, 0)
                slot_tile(2, 0, 1)
                with dve.Fori(1, NS // 2) as i:
                    slot_tile(2 * i + 1, 1, 2 * i)
                    slot_tile(2 * i + 2, 0, 2 * i + 1)
                copy_y(NS - 1, (NS - 1) % 2)

            nc.vector.memset(oneF[:], 1.0)
            nc.vector.memset(ones_b[:], 1.0).then_inc(consts_set, 1)
            nc.vector.memset(vp[:], 1.0).then_inc(vp_set, 1)
            def first_moments(b):
                dve.wait_ge(x_in[b], 16)
                moments(b, xn, stats, mv).then_inc(var_done, 1)

            first_moments(0)
            norm(0)
            first_moments(1)
            dve.wait_ge(xnT_full, 1)
            nc.vector.tensor_copy(xnT[:, 0:S], bank(0)).then_inc(xnT_done, 1)
            first_moments(2)
            low_part(0, 0, bank(4)).then_inc(lo_done, 1)
            first_moments(3)
            low_part(0, 1, bank(5)).then_inc(lo_done, 1)
            for b in range(1, B):
                norm(b)
            for b in range(B):
                moments(b, xn, stats, mv2).then_inc(var2_done, 1)
            for n in range(first_item(0)):
                maxima(n)
            for t in range(END + 1):
                if t == FFN_AT:
                    feed_forward()
                if t >= 1:
                    for kind, arg in tasks_at(t - 1):
                        task(kind, arg)
                if t < MAX_STEPS:
                    for n in range(first_item(t), first_item(t + 1)):
                        maxima(n)
                if t < PREFIX_AT:
                    routing(t)
                elif t > PREFIX_AT:
                    routing(t - 1)
                for b in range(B):
                    c = t - reciprocal_at(b)
                    if 0 <= c < QT:
                        if c == 0:
                            dve.wait_ge(gate_exp, b + 1)
                        gt = gtmp[:, b % 2, D * c:D * (c + 1)]
                        link(nc.vector.tensor_scalar(gt, gt, 1.0, None, ALU.add))
                        nc.vector.reciprocal(gt, gt).then_inc(gate_rec, 1)
                    if b not in ON_POOL and t == silu_at(b):
                        zb, sv = zrow[:, QT * b:QT * (b + 1), 0:D], s_of[b]
                        dve.wait_ge(gate_rec, QT * (b + 1))
                        nc.vector.tensor_tensor(zb, zb, gtmp[:, b % 2, :].rearrange("p (c d) -> p c d", d=D),
                                                ALU.mult).then_inc(gate_done[b], 1)
                        if b < B - 1:
                            dve.wait_ge(gate_done[b], 1)
                            dve.wait_ge(misc_empty, emptied("wo", b))
                            dve.wait_ge(x_again[b], 16)
                            link(nc.vector.tensor_tensor(sv, sv, zb, ALU.mult))
                            nc.vector.tensor_tensor(sv, sv, xn[:, QT * b:QT * (b + 1), :], ALU.add
                                                    ).then_inc(res_done[b], 1)

        @block.scalar
        def _(act):
            def values(b):
                act.wait_ge(v_full, b + 1)
                if b == 0:
                    act.wait_ge(vp_set, 1)
                o = QT * b * H * VW
                dst = vp[:, o:o + QT * H * VW].rearrange("p (c h w) -> p c h w", h=H, w=VW)
                src = ps[:, 6 + b % 2, :].rearrange("p (c h w) -> p c h w", h=H, w=DH)
                for c in range(QT):
                    last = nc.scalar.activation(dst[:, c, :, 0:DH], src[:, c, :, :], ACT.Copy)
                last.then_inc(v_done, 1)

            def high_part(b, which, src):
                if b >= 1 and which == 0:
                    pair, nr = 2 * b - 1, QRING // 2
                    for q in (pair - 1, pair):
                        act.wait_ge(q_placed[q % nr], 16 * 12 * (q // nr + 1))
                if b >= 1 and which == 1:
                    act.wait_ge(*k_placed_in(b - 1))
                nc.scalar.activation((qhl, khl)[which][:, 0, :], src, ACT.Copy).then_inc(hi_done, 1)

            def exponentials(t, j):
                u, kt = divmod(t, QT)
                lo, hi = q_tiles(kt)
                n = 4 * t + j
                act.wait_ge(st_full, n + 1)
                if j == 0 and t >= RING:
                    act.wait_ge(pv_done, t - RING + 1)
                nc.scalar.activation(probs[:, t % RING, j, 0:P * (hi - lo)], ps[:, st_bank(n), 0:P * (hi - lo)],
                                     ACT.Exp, scale=SCALE).then_inc(exp_done, 1)

            def copy_pv(u):
                act.wait_ge(pv_done, QT * (u + 1))
                if u == 1:
                    act.wait_ge(misc_full, number["aff_turn", 0] + 1)
                if u >= 2:
                    act.wait_ge(misc_full, number["o_turn", u - 2] + 1)
                nc.scalar.activation(oT[:, u % 2, :], bank(PV), ACT.Copy).then_inc(pv_copied, 1)

            def task(kind, arg):
                m = number[kind, arg]
                src = bank(MISC)
                if kind in ("q_proj", "k_proj"):
                    act.wait_ge(misc_full, m + 1)
                    high_part(arg, 0 if kind == "q_proj" else 1, src)
                elif kind == "max_t":
                    act.wait_ge(misc_full, m + 1)
                    if arg >= 2:
                        act.wait_ge(m_placed[(arg - 2) % QRING], 16 * ((arg - 2) // QRING + 1))
                    nc.scalar.activation(mT[:, arg % 2, :], src[0:4 * QT, 0:P], ACT.Copy).then_inc(misc_empty, 1)
                elif kind == "affinity":
                    act.wait_ge(misc_full, m + 1)
                    nc.scalar.activation(oT[:, 1, :], src, ACT.Copy).then_inc(misc_empty, 1)
                elif kind == "aff_turn":
                    act.wait_ge(misc_full, m + 1)
                    for qt in range(QT):
                        last = nc.scalar.activation(aff.rearrange("p (b q) e -> p q b e", q=QT)[:, qt, :, :],
                                                    src.rearrange("p (q b w) -> p q b w", b=B, w=32)[:, qt, :, 0:E],
                                                    ACT.Copy)
                    last.then_inc(misc_empty, 1)
                elif kind == "on_turn":
                    act.wait_ge(misc_full, m + 1)
                    if arg >= 1:
                        act.wait_ge(misc_full, number["wo", arg - 1] + 1)
                    nc.scalar.activation(onT[:], src, ACT.Copy).then_inc(misc_empty, 1)
                elif kind == "wo" and arg < B - 1:
                    act.wait_ge(misc_full, m + 1)
                    nc.scalar.activation(s_of[arg],
                                         src.rearrange("p (c d) -> p c d", d=D), ACT.Copy).then_inc(misc_empty, 1)

            def relu_half(j, par):
                act.wait_ge(h_full, j + 1)
                for c in range(FC // 2):
                    cc = c + FC // 2
                    last = nc.scalar.activation(hid[par][:, P * cc:P * (cc + 1)], ps[:, 2 * par + 1, P * c:P * (c + 1)],
                                                ACT.Relu, bias=stage1[par][:, F + cc:F + cc + 1])
                last.then_inc(h_act, 1)

            def expert_of(j):
                return act.value_load(expert[0:1, bass.ds(j, 1)], min_val=0, max_val=E - 1)

            def stage_2(e, par):
                nc.scalar.activation(stage2[par], wall_flat[:, bass.ds(e * WW + O_W2, ST2)], ACT.Copy
                                     ).then_inc(w2_staged, 1)

            def turned_rows(n):
                act.wait_ge(z_turned, n + 1)
                for c in range(4 * n, min(4 * n + 4, NS)):
                    last = nc.scalar.activation(zT[:, P * c:P * (c + 1)], ps[:, n, P * (c % 4):P * (c % 4) + P],
                                                ACT.Identity, scale=tile_gain[:, c:c + 1], bias=tile_bias[:, c:c + 1])
                last.then_inc(zT_act, 1)

            def slot_tile(j, par):
                e = expert_of(j + 1)
                relu_half(j, par)
                if not isinstance(j, int) or j >= 1:
                    act.wait_ge(y_copied, j)
                stage_2(e, 1 - par)

            act.wait_ge(qk0_full, 1)
            high_part(0, 0, bank(4))
            act.wait_ge(qk0_full, 2)
            high_part(0, 1, bank(5))
            values(0)
            for b in range(1, B):
                act.wait_ge(xnT_full, b + 1)
                nc.scalar.activation(xnT[:, S * b:S * (b + 1)], bank(b), ACT.Copy).then_inc(xnT_done, 1)
            for b in range(1, B):
                values(b)
            task("affinity", 0)
            task("aff_turn", 0)
            act.wait_ge(rstd2_done, 1)
            for c in range(NT):
                nc.scalar.activation(zrow[:, c, 0:D], xn[:, c, :], ACT.Identity, scale=rstd2[:, c:c + 1],
                                     bias=shift2[:, c:c + 1]).then_inc(z_done, 1)
                if c == NT // 2:
                    task("max_t", 0)
            for t in range(END + 1):
                if t == FFN_AT:
                    act.wait_ge(experts_done, 1)
                    e = [expert_of(j) for j in range(2)]
                    act.wait_ge(gain_made, 2)
                    turned_rows(1)
                    act.wait_ge(z_turned, TURNS)
                    act.wait_ge(dest_copied, 1)
                    act.wait_ge(w_in, 16 * (E + 1))
                    stage_2(e[0], 0)
                    turned_rows(3)
                    relu_half(0, 0)
                    stage_2(e[1], 1)
                    turned_rows(5)
                    with act.Fori(0, (NS - 1) // 2) as i:
                        slot_tile(2 * i + 1, 1)
                        slot_tile(2 * i + 2, 0)
                u, kt = divmod(t, QT)
                if t >= 1:
                    for kind, arg in tasks_at(t - 1):
                        task(kind, arg)
                for j in range(4):
                    if j == 0 and kt == 2 and 1 <= u <= UNITS:
                        copy_pv(u - 1)
                    if t < STEPS:
                        exponentials(t, j)
                if t == 1:
                    act.wait_ge(amax_done, 1)
                    nc.scalar.activation(ea[:], amax[:], ACT.Exp, scale=-1.0).then_inc(ea_done, 1)
                for b in range(B):
                    if t == gate_at(b):
                        act.wait_ge(gate_in, b + 1)
                        nc.scalar.activation(gtmp[:, b % 2, :].rearrange("p (c d) -> p c d", d=D),
                                             zrow[:, QT * b:QT * (b + 1), 0:D], ACT.Exp, scale=-1.0
                                             ).then_inc(gate_exp, 1)

        @block.gpsimd
        def _(pool):
            steps = [0]

            def link(ins):
                steps[0] += 1
                ins.then_inc(pool_step, 1)
                pool.wait_ge(pool_step, steps[0])

            def rsqrt(b, m, v, r, done):
                c = slice(QT * b, QT * (b + 1))
                link(nc.gpsimd.tensor_scalar(v[:, c], m[:, c, 1], EPS, None, ALU.add))
                nc.gpsimd.tensor_tensor(r[:, c], v[:, c], mhalf[:, c], ALU.pow).then_inc(done, 1)

            def mask(t):
                u, kt = divmod(t, QT)
                lo, hi = q_tiles(kt)
                pool.wait_ge(exp_done, 4 * t + 4)
                w = P * (hi - lo)
                last = None
                if kt > 0:
                    v = probs[:, t % RING, :, 0:P]
                    last = nc.gpsimd.affine_select(out=v, in_=v, compare_op=ALU.is_ge, fill=0.0, base=0,
                                                   pattern=[[0, 4], [1, P]], channel_multiplier=-1)
                    if kt == QT - 1:
                        last.then_inc(p_masked, 1)
                if kt < QT - 1:
                    v = probs[:, t % RING, :, w - P:w]
                    nc.gpsimd.affine_select(out=v, in_=v, compare_op=ALU.is_ge, fill=0.0, base=0,
                                            pattern=[[0, 4], [-1, P]], channel_multiplier=1).then_inc(p_masked, 1)

            def send_y(j, par):
                if not isinstance(j, int):
                    pool.wait_ge(y_sent[par], 8 * (j - par))
                elif j >= 2:
                    pool.wait_ge(y_sent[par], 16 * (j // 2))
                nc.gpsimd.tensor_copy(dest1[:, par, :], dest[:, bass.ds(j, 1)]).then_inc(dest_staged, 1)
                pool.wait_ge(dest_staged, j + 1)
                pool.wait_ge(y_copied, j + 1)
                pool.sem_inc(sending, 1)
                nc.gpsimd.indirect_dma_start(
                    out=f_dram, out_offset=bass.IndirectOffsetOnAxis(ap=dest1[:, par, :].bitcast(U32), axis=0),
                    in_=ysb[:, par, :], in_offset=None).then_inc(y_sent[par], 16)

            def feed_forward():
                send_y(0, 0)
                send_y(1, 1)
                with pool.Fori(1, NS // 2) as i:
                    send_y(2 * i, 0)
                    send_y(2 * i + 1, 1)
                send_y(NS - 1, (NS - 1) % 2)

            nc.gpsimd.memset(mhalf[:], -0.5).then_inc(pool_step, 1)
            steps[0] += 1
            pool.wait_ge(pool_step, steps[0])
            def clear_q(r):
                nc.gpsimd.memset(raw(qst[:, 2 * r:2 * r + 2, :, :]), 0.0).then_inc(qst_zero, 1)

            def first_rstd(b):
                pool.wait_ge(var_done, b + 1)
                rsqrt(b, mv, vare, rstd, rstd_done)

            clear_q(0)
            first_rstd(0)
            clear_q(1)
            for b in range(1, B):
                first_rstd(b)
            pool.wait_ge(hi_done, 2)
            k_slots(pool, 0, K_HI)
            pool.wait_ge(lo_done, 2)
            k_slots(pool, 0, K_LO)
            pool.wait_ge(rstd_done, B)
            nc.gpsimd.memset(raw(kst[96:97, :, :, :]), 1.0).then_inc(kst_ones, 1)
            pool.wait_ge(kst_ones, 1)
            pool.wait_ge(var2_done, B)
            link(nc.gpsimd.tensor_scalar(vare[:], mv2[:, :, 1], EPS, None, ALU.add))
            link(nc.gpsimd.tensor_tensor(rstd2[:], vare[:], mhalf[:], ALU.pow))
            link(nc.gpsimd.tensor_tensor(shift2[:], mv2[:, :, 0], rstd2[:], ALU.mult))
            nc.gpsimd.tensor_scalar(shift2[:], shift2[:], -1.0, None, ALU.mult).then_inc(rstd2_done, 1)
            clear_q(2)
            link(nc.gpsimd.memset(before[:], 1.0))
            nc.gpsimd.affine_select(out=before[:], in_=before[:], compare_op=ALU.is_gt, fill=0.0, base=0,
                                    pattern=[[1, P]], channel_multiplier=-1).then_inc(consts_set, 1)
            nc.gpsimd.iota(firstw[:], [[-1, E]], base=E, channel_multiplier=0,
                           allow_small_or_imprecise_dtypes=True).then_inc(consts_set, 1)
            pool.wait_ge(consts_set, 3)
            nc.gpsimd.iota(starts[:], [[P, NX], [0, E]], base=0, channel_multiplier=0,
                           allow_small_or_imprecise_dtypes=True).then_inc(consts_set, 1)
            pool.wait_ge(consts_set, 4)
            nc.gpsimd.iota(zrow[:, :, D:ROW].bitcast(I32), [[P, NT], [0, 1]], base=0, channel_multiplier=1
                           ).then_inc(consts_set, 1)
            nc.gpsimd.memset(zs[:, :, 0:D], 0.0).then_inc(pre_made, 1)
            nc.gpsimd.iota(zs[:, :, D:ROW].bitcast(I32), [[P, NS], [0, 1]], base=T, channel_multiplier=1
                           ).then_inc(pre_made, 1)
            for t in range(END + 1):
                if t < STEPS:
                    if t == FFN_AT:
                        feed_forward()
                    mask(t)
                c = t - SEND_AT
                if 0 <= c < NT:
                    if c == 0:
                        pool.wait_ge(slots_done, 1)
                        pool.wait_ge(z_done, NT)
                        pool.wait_ge(z_cleared, 16)
                        pool.wait_ge(consts_set, 5)
                    nc.gpsimd.indirect_dma_start(
                        out=z_dram, out_offset=bass.IndirectOffsetOnAxis(ap=slot[:, c:c + 1].bitcast(U32), axis=0),
                        in_=zrow[:, c, :], in_offset=None).then_inc(z_sent, 16)
                if t == FFN_AT - 1:
                    pool.wait_ge(zs_in, 16)
                    nc.gpsimd.tensor_copy(dest[:].unsqueeze(2), zs[:, :, D:ROW].bitcast(I32)).then_inc(dest_copied, 1)
                    pool.wait_ge(dest_copied, 1)
                for b in range(B):
                    zb = zrow[:, QT * b:QT * (b + 1), 0:D]
                    gt = gtmp[:, b % 2, :].rearrange("p (c d) -> p c d", d=D)
                    if t == gate_at(b) - 3:
                        pool.wait_ge(f_in[b], 16)
                        pool.wait_ge(alpha_done, 1)
                        al = alpha[:, QT * b:QT * (b + 1)].unsqueeze(2).broadcast_to([P, QT, D])
                        link(nc.gpsimd.tensor_tensor(zb, zb, al, ALU.mult))
                    if t == gate_at(b) - 2:
                        nc.gpsimd.tensor_tensor(zb, zb, xn[:, QT * b:QT * (b + 1), :], ALU.add).then_inc(gate_in, 1)
                    if t == silu_at(b) and b in ON_POOL:
                        pool.wait_ge(gate_rec, QT * (b + 1))
                        nc.gpsimd.tensor_tensor(zb, zb, gt, ALU.mult).then_inc(gate_done[b], 1)
                    if b in ON_POOL:
                        sv = s_of[b]
                        if t == silu_at(b) + 1:
                            pool.wait_ge(misc_empty, emptied("wo", b))
                            pool.wait_ge(gate_done[b], 1)
                            link(nc.gpsimd.tensor_tensor(sv, sv, zb, ALU.mult))
                        if t == silu_at(b) + 3:
                            pool.wait_ge(x_again[b], 16)
                            nc.gpsimd.tensor_tensor(sv, sv, xn[:, QT * b:QT * (b + 1), :], ALU.add
                                                    ).then_inc(res_done[b], 1)


_INS = ["x", "w_attn", "small", "w_ffn", "b2", "ident_in"]


def kernel(**inputs):
    import numpy as np
    import concourse.bacc as bacc
    from concourse.bass_utils import run_bass_kernel_spmd as run

    a = {k.split("_", 1)[1]: np.asarray(v) for k, v in inputs.items()}
    x = a["attn_x"]
    E, F, D = a["ffn_w1"].shape
    wq = a["attn_Wq"].reshape(2, 2, 4, 8, D).transpose(0, 2, 3, 1, 4).reshape(D, D)
    wk = a["attn_Wk"].reshape(4, 4, 8, D).transpose(1, 2, 0, 3).reshape(D, D)
    w1 = a["ffn_w1"].transpose(2, 0, 1)
    b1 = a["ffn_b1"].reshape(E, F // 128, 128).transpose(2, 0, 1)
    w2 = a["ffn_w2"].reshape(E, D, F // 128, 128).transpose(3, 0, 2, 1).reshape(128, E, F // 128 * D)
    laid = {
        "x": x.reshape(-1, D),
        "w_attn": np.stack([w.T for w in (wq, wk, a["attn_Wv"], a["attn_Wo"])], 1),
        "small": np.stack([a["ffn_centroids"].T, a["ffn_ln_g"].T, a["ffn_ln_b"].T, a["ffn_centroids"].T], 1),
        "w_ffn": np.concatenate([w1, b1, w2], 2),
        "b2": a["ffn_b2"],
        "ident_in": np.eye(128, dtype=np.float32),
    }
    nc = bacc.Bacc("TRN2", target_bir_lowering=False, num_devices=1)
    arrays, args = {}, []
    for name in _INS:
        v = np.ascontiguousarray(laid[name])
        arrays[f"in_{name}_dram"] = v
        args.append(nc.dram_tensor(f"in_{name}_dram", v.shape, mybir.dt.from_np(v.dtype), kind="ExternalInput").ap())
    args.append(nc.dram_tensor("out_0_dram", (x.shape[0] * x.shape[1], D), F32, kind="ExternalOutput").ap())
    build(nc, *args)
    r = run(nc, [arrays], core_ids=[0])
    return r.results[0]["out_0_dram"].reshape(x.shape)
```
